# Optimizing a Trainium2 kernel written in Bass

```python
import numpy as np
import jax
import jax.numpy as jnp

def _softmax(x, axis=-1):
    return jax.nn.softmax(x, axis=axis)

def _gelu(x):
    return jax.nn.gelu(x, approximate=True)

def _silu(x):
    return jax.nn.silu(x)

def _sigmoid(x):
    return jax.nn.sigmoid(x)

def _layernorm(x, axis=-1, eps=1e-05):
    m = jnp.mean(x, axis=axis, keepdims=True)
    v = jnp.var(x, axis=axis, keepdims=True)
    return (x - m) / jnp.sqrt(v + eps)

def _scatter_add(tgt, idx, src, axis=0):
    return tgt.at[idx].add(src)

def _segment_sum(src, seg, n):
    return jax.ops.segment_sum(src, seg, n)
kernel_name = 'mk_seq_postln_d1_jaxref_r4_f42767'

def setup_inputs(seed: int=0):
    np.random.seed(seed)
    _w = jnp.asarray

    def _L0_attn_setup():
        import jax, jax.numpy as jnp
        import numpy as np
        from jax import lax
        H = 16
        MB = 16
        LR = 1.0
        ROPE_BASE = 10000.0
        LN_EPS = 1e-05

        def _rotate_half(u):
            u1, u2 = jnp.split(u, 2, axis=-1)
            return jnp.concatenate([-u2, u1], axis=-1)
        key = jax.random.key(seed)
        ks = jax.random.split(key, 4)
        B, S, D = (4, 1024, 512)
        x = jax.random.normal(ks[0], (B, S, D), dtype=jnp.float32)
        scale = 1.0 / np.sqrt(D)
        Wk = jax.random.normal(ks[1], (D, D), dtype=jnp.float32) * scale
        Wv = jax.random.normal(ks[2], (D, D), dtype=jnp.float32) * scale
        Wo = jax.random.normal(ks[3], (D, D), dtype=jnp.float32) * scale
        ln_gamma = jnp.ones((D,), dtype=jnp.float32)
        ln_beta = jnp.zeros((D,), dtype=jnp.float32)
        return {'x': x, 'Wk': Wk, 'Wv': Wv, 'Wo': Wo, 'ln_gamma': ln_gamma, 'ln_beta': ln_beta}
    _L0_attn_in = _L0_attn_setup()

    def _L0_ffn_setup():
        import jax, jax.numpy as jnp
        import numpy as np
        HIDDEN = 512
        INTER = 1408
        B, S = (2, 512)

        def _ternary(key, shape):
            return jax.random.randint(key, shape, -1, 2).astype(jnp.float32)
        key = jax.random.key(seed)
        ks = jax.random.split(key, 7)
        x = jax.random.normal(ks[0], (B, S, HIDDEN), dtype=jnp.float32)
        gate_w = _ternary(ks[1], (INTER, HIDDEN))
        up_w = _ternary(ks[2], (INTER, HIDDEN))
        down_w = _ternary(ks[3], (HIDDEN, INTER))
        gate_s = jax.random.uniform(ks[4], (INTER,), minval=0.01, maxval=0.1, dtype=jnp.float32)
        up_s = jax.random.uniform(ks[5], (INTER,), minval=0.01, maxval=0.1, dtype=jnp.float32)
        down_s = jax.random.uniform(ks[6], (HIDDEN,), minval=0.01, maxval=0.1, dtype=jnp.float32)
        return {'x': x, 'gate_w': gate_w, 'up_w': up_w, 'down_w': down_w, 'gate_s': gate_s, 'up_s': up_s, 'down_s': down_s}
    _L0_ffn_in = _L0_ffn_setup()
    _d = {'L0_attn_x': _L0_attn_in['x'], 'L0_attn_Wk': _L0_attn_in['Wk'], 'L0_attn_Wv': _L0_attn_in['Wv'], 'L0_attn_Wo': _L0_attn_in['Wo'], 'L0_attn_ln_gamma': _L0_attn_in['ln_gamma'], 'L0_attn_ln_beta': _L0_attn_in['ln_beta'], 'L0_ffn_gate_w': _L0_ffn_in['gate_w'], 'L0_ffn_up_w': _L0_ffn_in['up_w'], 'L0_ffn_down_w': _L0_ffn_in['down_w'], 'L0_ffn_gate_s': _L0_ffn_in['gate_s'], 'L0_ffn_up_s': _L0_ffn_in['up_s'], 'L0_ffn_down_s': _L0_ffn_in['down_s']}
    _x0 = _d['L0_attn_x']
    _d['L0_attn_x'] = jax.random.normal(jax.random.fold_in(jax.random.key(seed), 1), (2, 4096, 512), dtype=_x0.dtype)
    del _x0
    return _d

def reference(L0_attn_x, L0_attn_Wk, L0_attn_Wv, L0_attn_Wo, L0_attn_ln_gamma, L0_attn_ln_beta, L0_ffn_gate_w, L0_ffn_up_w, L0_ffn_down_w, L0_ffn_gate_s, L0_ffn_up_s, L0_ffn_down_s):

    def _L0_attn_ref(x, Wk, Wv, Wo, ln_gamma, ln_beta):
        import jax, jax.numpy as jnp
        import numpy as np
        from jax import lax
        H = 16
        MB = 16
        LR = 1.0
        ROPE_BASE = 10000.0
        LN_EPS = 1e-05

        def _rotate_half(u):
            u1, u2 = jnp.split(u, 2, axis=-1)
            return jnp.concatenate([-u2, u1], axis=-1)
        B, S, Dm = x.shape
        Dh = Dm // H
        k = (x @ Wk.T).reshape(B, S, H, Dh).transpose(0, 2, 1, 3)
        v = (x @ Wv.T).reshape(B, S, H, Dh).transpose(0, 2, 1, 3)
        inv_freq = 1.0 / ROPE_BASE ** (jnp.arange(0, Dh, 2, dtype=jnp.float32) / Dh)
        t = jnp.arange(S, dtype=jnp.float32)
        freqs = t[:, None] * inv_freq[None, :]
        emb = jnp.concatenate([freqs, freqs], axis=-1)
        cos, sin = (jnp.cos(emb), jnp.sin(emb))
        k = k * cos + _rotate_half(k) * sin
        nmb = S // MB
        k_c = k.reshape(B, H, nmb, MB, Dh).transpose(2, 0, 1, 3, 4)
        v_c = v.reshape(B, H, nmb, MB, Dh).transpose(2, 0, 1, 3, 4)
        W0 = jnp.broadcast_to(jnp.eye(Dh, dtype=x.dtype), (B, H, Dh, Dh))
        inv_n = 2.0 / (MB * Dh)

        def step(W, kv):
            kc, vc = kv
            z = jnp.einsum('bhsd,bhde->bhse', kc, W)
            grad = jnp.einsum('bhsd,bhse->bhde', kc, (z - vc) * inv_n)
            return (W - LR * grad, z)
        _, zs = lax.scan(step, W0, (k_c, v_c))
        out = zs.transpose(1, 2, 0, 3, 4).reshape(B, H, S, Dh)
        out = out.transpose(0, 2, 1, 3).reshape(B, S, Dm)
        mu = jnp.mean(out, axis=-1, keepdims=True)
        var = jnp.var(out, axis=-1, keepdims=True)
        out = (out - mu) * lax.rsqrt(var + LN_EPS) * ln_gamma + ln_beta
        return out @ Wo.T

    def _L0_ffn_ref(x, gate_w, up_w, down_w, gate_s, up_s, down_s):
        import jax, jax.numpy as jnp
        import numpy as np
        HIDDEN = 512
        INTER = 1408
        B, S = (2, 512)

        def _ternary(key, shape):
            return jax.random.randint(key, shape, -1, 2).astype(jnp.float32)
        b, s, h = x.shape
        xf = x.reshape(b * s, h)
        g = jnp.einsum('th,ih->ti', xf, gate_w) * gate_s
        u = jnp.einsum('th,ih->ti', xf, up_w) * up_s
        hdn = jax.nn.silu(g) * u
        out = jnp.einsum('ti,hi->th', hdn, down_w) * down_s
        return out.reshape(b, s, -1)
    x = L0_attn_x
    x = _layernorm(x + _L0_attn_ref(x, L0_attn_Wk, L0_attn_Wv, L0_attn_Wo, L0_attn_ln_gamma, L0_attn_ln_beta), axis=-1)
    x = _layernorm(x + _L0_ffn_ref(x, L0_ffn_gate_w, L0_ffn_up_w, L0_ffn_down_w, L0_ffn_gate_s, L0_ffn_up_s, L0_ffn_down_s), axis=-1)
    return x

_drawn_inputs = setup_inputs


def setup_inputs(seed=0):
    import zlib

    import numpy as np

    out = dict(_drawn_inputs(seed))
    spreads = {'L0_attn_ln_gamma': (1.0, 0.2), 'L0_attn_ln_beta': (0.0, 0.1)}
    factors = {}
    for name, (base, spread) in spreads.items():
        noise = np.random.default_rng([zlib.crc32(name.encode()), seed]).standard_normal(out[name].shape)
        drawn = base * np.exp(spread * noise) if base else spread * noise
        out[name] = jnp.asarray(drawn.astype(out[name].dtype))
    for name, factor in factors.items():
        out[name] = (out[name] * factor).astype(out[name].dtype)
    return out
```

```python
from contextlib import ExitStack

import numpy as np

import concourse.bass as bass
from concourse import mybir

F32 = mybir.dt.float32
ACT = mybir.ActivationFunctionType
ALU = mybir.AluOpType

P = 128
BATCH, SEQ, DM = 2, 4096, 512
HEAD = 32
MB = 16
NC = DM // P
NG = BATCH * NC
HQ = P // HEAD
NT = SEQ // P
NS = P // MB
INTER = 1408
NM = INTER // P
TOK = BATCH * P
RING = 3
SLOTS = 2 * NS
LN_EPS = 1e-5
STEP = 2.0 / (MB * HEAD)
assert STEP == 2.0 ** -8 and NG * MB == P and NT % 2 == 0


class Nth:

    def __init__(self, off, reg=None):
        self.off, self.reg = off, reg

    def back(self, d):
        return Nth(self.off - d, self.reg)

    def count(self, per, more=0):
        c = per * self.off + more
        return c if self.reg is None else self.reg * (2 * per) + c

    def turn(self, per, more=0):
        c = per * (self.off // 2) + more
        return c if self.reg is None else self.reg * per + c

    def past(self, k):
        return self.reg is not None or self.off >= k

    @property
    def par(self):
        return self.off % 2

    def within(self):
        return self.reg is not None or 0 <= self.off < NT


def build(nc, xT, x, wkT, wvT, woT, gamma, beta, gwT, uwT, dwT, gs, us, ds_row, rope, ident, ident_rep, out):
    with ExitStack() as ctx:
        def sb(name, shape, dt=F32):
            return ctx.enter_context(nc.sbuf_tensor(name, shape, dt))

        def sem(name):
            return ctx.enter_context(nc.semaphore(name))

        k_scr = nc.dram_tensor("k_scr", [BATCH, P, DM], F32, kind="Internal").ap()
        v_scr = nc.dram_tensor("v_scr", [BATCH, P, DM], F32, kind="Internal").ap()
        z_scr = nc.dram_tensor("z_scr", [BATCH, SEQ, DM], F32, kind="Internal").ap()

        wk = sb("wk", [P, NC, DM])
        wv = sb("wv", [P, NC, DM])
        wo = sb("wo", [P, NC, DM])
        gw = sb("gw", [P, NC, INTER])
        uw = sb("uw", [P, NC, INTER])
        dw = sb("dw", [P, NM, DM])
        gate_scale = sb("gate_scale", [P, NM])
        up_scale = sb("up_scale", [P, NM])
        down_scale = sb("down_scale", [P, DM])
        ln_gamma = sb("ln_gamma", [P, NC])
        ln_beta = sb("ln_beta", [P, NC])
        eye = sb("eye", [P, P])
        eye_rep = sb("eye_rep", [P, NG, HEAD])
        neg_half = sb("neg_half", [P, BATCH])
        x_fm = [sb(f"x_fm{i}", [P, NC, BATCH, P]) for i in range(2)]
        rot = [sb(f"rot{i}", [P, 2, HEAD]) for i in range(2)]
        k_tok = sb("k_tok", [P, BATCH, DM])
        k_sin = sb("k_sin", [P, BATCH, DM])
        v_tok = sb("v_tok", [P, BATCH, DM])
        k_rows = [sb(f"k_rows{i}", [P, NS, P]) for i in range(2)]
        v_rows = [sb(f"v_rows{i}", [P, NS, 2, P]) for i in range(2)]
        k_cols = [sb(f"k_cols{i}", [P, NG, NS, 2 * MB]) for i in range(2)]
        err = sb("err", [P, NG, HQ, HEAD])
        state = sb("state", [P, NG, P])
        z_rows = sb("z_rows", [P, NS, 2 * P])
        z_tok = sb("z_tok", [P, BATCH, DM])
        zn_fm = sb("zn_fm", [P, NC, BATCH, P])
        x_tok = sb("x_tok", [P, BATCH, DM])
        x1_tok = [sb(f"x1_tok{i}", [P, BATCH, DM]) for i in range(2)]
        x1_fm = sb("x1_fm", [P, NC, BATCH, P])
        silu_g = [sb(f"silu_g{i}", [P, TOK]) for i in range(2)]
        hid = [sb(f"hid{i}", [P, TOK]) for i in range(RING)]
        y_tok = sb("y_tok", [P, BATCH, DM])
        stats = sb("stats", [P, 3, BATCH, 6])
        moments = sb("moments", [P, 3, BATCH, 2])
        var_eps = sb("var_eps", [P, 3, BATCH])
        spare = sb("spare", [P, 1])
        rstd = sb("rstd", [P, 3, BATCH])

        def bank(name):
            return ctx.enter_context(nc.psum_tensor(name, [P, 512], F32))

        state_acc = bank("state_acc")
        z_acc = bank("z_acc")
        gu_acc = [bank("gu_acc0"), bank("gu_acc1")]
        down_acc = [bank("down_acc0"), bank("down_acc1")]
        work = [bank("work0"), bank("work1")]

        w_in = sem("w_in")
        wo_in = sem("wo_in")
        ffn_in = sem("ffn_in")
        small_in = sem("small_in")
        zeroed = sem("zeroed")
        x_fm_in = [sem("x_fm_in0"), sem("x_fm_in1")]
        k_projected = sem("k_projected")
        v_projected = sem("v_projected")
        k_mul = sem("k_mul")
        k_ready = sem("k_ready")
        v_ready = sem("v_ready")
        k_stored = sem("k_stored")
        v_stored = sem("v_stored")
        rows_in = sem("rows_in")
        k_turned = sem("k_turned")
        k_cols_ready = sem("k_cols_ready")
        state_begun = sem("state_begun")
        z_done = sem("z_done")
        z_saved = sem("z_saved")
        err_ready = sem("err_ready")
        state_added = sem("state_added")
        state_ready = sem("state_ready")
        z_stored = sem("z_stored")
        z_tok_in = sem("z_tok_in")
        x_tok_in = sem("x_tok_in")
        stats_done = [sem(f"stats_done{i}") for i in range(3)]
        moments_done = [sem(f"moments_done{i}") for i in range(3)]
        var_done = [sem(f"var_done{i}") for i in range(3)]
        rstd_done = [sem(f"rstd_done{i}") for i in range(3)]
        zn_ready = sem("zn_ready")
        zn_turned = sem("zn_turned")
        zn_fm_ready = sem("zn_fm_ready")
        o_done = sem("o_done")
        o_added = sem("o_added")
        x1_ready = sem("x1_ready")
        x1_turned = sem("x1_turned")
        x1_fm_ready = sem("x1_fm_ready")
        gu_done = sem("gu_done")
        silu_done = sem("silu_done")
        hid_ready = sem("hid_ready")
        down_done = sem("down_done")
        y_scaled = sem("y_scaled")
        y_added = sem("y_added")
        y_ready = sem("y_ready")
        out_stored = sem("out_stored")

        block = ctx.enter_context(nc.Block())

        FIRST, LAST = 4, NT - 2

        def run(eng, tick):
            for t in range(FIRST):
                tick(Nth(t))
            with eng.Fori(FIRST // 2, LAST // 2) as pair:
                tick(Nth(0, pair))
                tick(Nth(1, pair))
            for t in range(LAST, NT + 3):
                tick(Nth(t))

        def rows(n, b=None, first=0, count=P):
            return bass.ds(n.count(P, first), count)

        @block.sync
        def _(sp):
            sp.dma_start(wk[:], wkT.rearrange("(c p) n -> p c n", p=P)).then_inc(w_in, 16)

            def ahead(value):
                if not isinstance(value, int):
                    sp.compute_val(value)
                return value

            def load_x_fm(n, used):
                if n.past(2):
                    sp.wait_ge(v_projected, used)
                for b in range(BATCH):
                    sp.dma_start(x_fm[n.par][:, :, b, :],
                                 xT[:, b, rows(n)].rearrange("(c p) t -> p c t", p=P)).then_inc(x_fm_in[n.par], 16)
                sp.dma_start(rot[n.par][:], rope[rows(n), :].rearrange("t (a d) -> t a d", a=2)
                             ).then_inc(x_fm_in[n.par], 16)

            load_x_fm(Nth(0), 0)
            sp.dma_start(wv[:], wvT.rearrange("(c p) n -> p c n", p=P)).then_inc(w_in, 16)
            for dst, src in ((gate_scale, gs), (up_scale, us), (down_scale, ds_row), (ln_gamma, gamma),
                             (ln_beta, beta), (eye, ident)):
                sp.dma_start(dst[:], src).then_inc(small_in, 16)
            sp.dma_start(eye_rep[:], ident_rep.rearrange("p (g e) -> p g e", g=NG)).then_inc(small_in, 16)
            sp.dma_start(wo[:], woT.rearrange("(c p) n -> p c n", p=P)).then_inc(wo_in, 16)
            for dst, src in ((gw, gwT), (uw, uwT), (dw, dwT)):
                sp.dma_start(dst[:], src.rearrange("(c p) n -> p c n", p=P)).then_inc(ffn_in, 16)
            sp.wait_ge(zeroed, 7)

            def store_z(n, half, saved, stored):
                i0 = half * NS // 2
                sp.wait_ge(z_saved, saved)
                for g in range(NG):
                    b, hg = divmod(g, NC)
                    sp.dma_start(z_scr[b, rows(n, first=i0 * MB, count=P // 2), hg * P:(hg + 1) * P]
                                 .rearrange("(i t) c -> t i c", t=MB),
                                 z_rows[g * MB:(g + 1) * MB, i0:i0 + NS // 2, (g % 2) * P:(g % 2 + 1) * P]
                                 ).then_inc(z_stored, 16)
                sp.wait_ge(z_stored, stored)

            def tick(t):
                nb, ncc, nd = t.back(1), t.back(2), t.back(3)
                saved = [ahead(n.count(NS, (half + 1) * NS // 2)) for half, n in enumerate((nb, ncc))]
                z_sent = [ahead(n.count(2 * 16 * NG, (half + 1) * 16 * NG)) for half, n in enumerate((nb, ncc))]
                c_before, x_used, both = ahead(ncc.count(2)), ahead(t.count(2)), ahead(t.count(2, 2))
                scanned, kv_sent = ahead(t.count(4 * NS, -4 * NS)), ahead(t.count(16, 16))
                rows_sent, y_both = ahead(t.count(32 * NG, 32 * NG)), ahead(nd.count(2, 2))
                if ncc.within():
                    store_z(ncc, 1, saved[1], z_sent[1])
                    if ncc.past(1):
                        sp.wait_ge(zn_turned, c_before)
                        sp.wait_ge(x1_ready, c_before)
                    sp.dma_start(z_tok[:], z_scr[:, rows(ncc), :].rearrange("b t f -> t b f")).then_inc(z_tok_in, 16)
                    sp.dma_start(x_tok[:], x[:, rows(ncc), :].rearrange("b t f -> t b f")).then_inc(x_tok_in, 16)
                if t.back(-1).within():
                    load_x_fm(t.back(-1), x_used)
                if t.within():
                    sp.wait_ge(k_ready, both)
                    sp.dma_start(k_scr.rearrange("b t f -> t b f"), k_tok[:]).then_inc(k_stored, 16)
                    sp.wait_ge(v_ready, both)
                    sp.dma_start(v_scr.rearrange("b t f -> t b f"), v_tok[:]).then_inc(v_stored, 16)
                    if t.past(2):
                        sp.wait_ge(state_added, scanned)
                    for scr, stored in ((k_scr, k_stored), (v_scr, v_stored)):
                        sp.wait_ge(stored, kv_sent)
                        for g in range(NG):
                            b, hg = divmod(g, NC)
                            r = slice(g * MB, (g + 1) * MB)
                            dst = k_rows[t.par][r] if scr is k_scr else v_rows[t.par][r, :, g % 2, :]
                            sp.dma_start(dst, scr[b, :, hg * P:(hg + 1) * P].rearrange("(i t) c -> t i c", t=MB)
                                         ).then_inc(rows_in, 16)
                    sp.wait_ge(rows_in, rows_sent)
                if nb.within():
                    store_z(nb, 0, saved[0], z_sent[0])
                if nd.within():
                    sp.wait_ge(y_ready, y_both)
                    sp.dma_start(out[:, rows(nd), :].rearrange("b t f -> t b f"), y_tok[:]).then_inc(out_stored, 16)

            run(sp, tick)
            sp.wait_ge(out_stored, 16 * NT)

        @block.gpsimd
        def _(pool):
            for buf in (*v_rows, *k_cols, err, state):
                pool.memset(buf[:], 0.0).then_inc(zeroed, 1)
            pool.memset(neg_half[:], -0.5).then_inc(zeroed, 1)
            pool.wait_ge(zeroed, 7)

            def inverse_root(norm, n):
                pool.wait_ge(var_done[norm], n.count(1, 1))
                pool.tensor_tensor(rstd[:, norm, :], var_eps[:, norm, :], neg_half[:], ALU.pow
                                   ).then_inc(rstd_done[norm], 1)

            def tick(t):
                if t.within():
                    for b in range(BATCH):
                        pool.wait_ge(k_mul, t.count(6, 3 * b + 3))
                        pool.tensor_tensor(k_tok[:, b, :], k_tok[:, b, :], k_sin[:, b, :], ALU.add
                                           ).then_inc(k_ready, 1)
                if t.back(2).within():
                    inverse_root(0, t.back(2))
                    inverse_root(1, t.back(2))
                if t.back(3).within():
                    inverse_root(2, t.back(3))

            run(pool, tick)

        @block.scalar
        def _(act):
            def copy_state():
                for h in range(HQ):
                    q = slice(h * HEAD, (h + 1) * HEAD)
                    act.activation(state[q, :, q], state_acc[q, 0:NG * HEAD].rearrange("p (g e) -> p g e", g=NG),
                                   ACT.Copy, scale=-STEP).then_inc(state_ready, 1)

            act.wait_ge(zeroed, 7)
            act.wait_ge(state_begun, HQ)
            copy_state()
            act.wait_ge(small_in, 16 * 7)

            def tick(t):
                nb, ncc, nd = t.back(1), t.back(2), t.back(3)
                for s in range(SLOTS):
                    i = s // 2
                    if nb.within() and s % 2 == 0:
                        act.wait_ge(err_ready, nb.count(4 * NS, 4 * i + 4))
                        if nb.past(1):
                            act.wait_ge(z_stored, nb.count(32 * NG, -32 * NG + 16 * NG * (1 + i // (NS // 2))))
                        act.activation(z_rows[:, i, :], z_acc[:, 0:2 * P], ACT.Copy
                                       ).then_inc(z_saved, 1)
                    if nb.within() and s % 2 == 1:
                        act.wait_ge(state_added, nb.count(4 * NS, 4 * i + 4))
                        copy_state()
                    if nd.within() and s < NM:
                        act.wait_ge(gu_done, nd.count(NM, s + 1))
                        if s >= 2 or nd.past(1):
                            act.wait_ge(hid_ready, nd.count(NM, s - 1))
                        act.activation(silu_g[s % 2][:], gu_acc[s % 2][:, 0:TOK], ACT.Silu,
                                       scale=gate_scale[:, s:s + 1]).then_inc(silu_done, 1)
                    if t.within() and s in (4, 5):
                        b = s - 4
                        act.wait_ge(v_projected, t.count(2, b + 1))
                        if t.past(1):
                            act.wait_ge(v_stored, t.count(16))
                        act.activation(v_tok[:, b, :], work[b][:], ACT.Copy).then_inc(v_ready, 1)
                    if ncc.within() and s == 6:
                        for b in range(BATCH):
                            act.wait_ge(zn_turned, ncc.count(2, b + 1))
                            if ncc.past(1):
                                act.wait_ge(o_done, ncc.count(2))
                            for c in range(NC):
                                act.activation(zn_fm[:, c, b, :], work[b][:, c * P:(c + 1) * P], ACT.Identity,
                                               scale=ln_gamma[:, c:c + 1], bias=ln_beta[:, c:c + 1]
                                               ).then_inc(zn_fm_ready, 1)
                    if ncc.within() and s in (12, 13):
                        b = s - 12
                        act.wait_ge(x1_turned, ncc.count(2, b + 1))
                        if ncc.past(1):
                            act.wait_ge(gu_done, ncc.count(NM))
                        act.activation(x1_fm[:, :, b, :], work[b][:].rearrange("p (c t) -> p c t", c=NC), ACT.Copy
                                       ).then_inc(x1_fm_ready, 1)

            run(act, tick)

        @block.tensor
        def _(pe):
            pe.wait_ge(small_in, 16 * 7)
            pe.wait_ge(zeroed, 7)
            for h in range(HQ):
                q = slice(h * HEAD, (h + 1) * HEAD)
                pe.matmul(state_acc[q, 0:NG * HEAD], lhsT=eye[:, q], rhs=eye_rep[:], start=True, stop=False,
                          skip_group_check=True, tile_position=(0, h * HEAD)).then_inc(state_begun, 1)
            pe.wait_ge(w_in, 32)

            def scan_z(n, i):
                if i == 0:
                    pe.wait_ge(rows_in, n.count(32 * NG, 32 * NG))
                    pe.wait_ge(k_cols_ready, n.count(4, 4))
                pe.wait_ge(state_ready, n.count(4 * NS, 4 * i + 4))
                if i >= 1 or n.past(1):
                    pe.wait_ge(z_saved, n.count(NS, i))
                for g in range(NG):
                    j = g // 2
                    mm = pe.matmul(z_acc[j * HEAD:(j + 1) * HEAD, g % 2 * P:(g % 2 + 1) * P],
                                   lhsT=k_cols[n.par][:, g, i, :], rhs=state[:, g, :], start=True, stop=True,
                                   skip_group_check=True, tile_position=(0, j * HEAD))
                    if g % 2:
                        mm.then_inc(z_done, 1)

            def scan_state(n, i):
                pe.wait_ge(err_ready, n.count(4 * NS, 4 * i + 4))
                for h in range(HQ):
                    q = slice(h * HEAD, (h + 1) * HEAD)
                    pe.matmul(state_acc[q, 0:NG * HEAD], lhsT=k_rows[n.par][:, i, q], rhs=err[:, :, h, :],
                              start=False, stop=False, skip_group_check=True, tile_position=(0, h * HEAD)
                              ).then_inc(state_added, 1)

            def project(n, b, w, done):
                for c in range(NC):
                    mm = pe.matmul(work[b][:], lhsT=x_fm[n.par][:, c, b, :], rhs=w[:, c, :],
                                   start=(c == 0), stop=(c == NC - 1))
                mm.then_inc(done, 1)

            def turn(src, b, done):
                for c in range(NC):
                    mm = pe.transpose(work[b][:, c * P:(c + 1) * P], src[:, b, c * P:(c + 1) * P], eye[:])
                mm.then_inc(done, 1)

            def tick(t):
                nb, ncc, nd = t.back(1), t.back(2), t.back(3)
                for s in range(SLOTS):
                    if nb.within():
                        if s % 2 == 0:
                            scan_z(nb, s // 2)
                        else:
                            scan_state(nb, s // 2)
                    if nd.within() and s < NM:
                        if s == 0:
                            pe.wait_ge(x1_fm_ready, nd.count(2, 2))
                            if not nd.past(1):
                                pe.wait_ge(ffn_in, 48)
                        if s >= 2 or nd.past(1):
                            pe.wait_ge(hid_ready, nd.count(NM, s - 1))
                        for k, w in enumerate((gw, uw)):
                            for c in range(NC):
                                mm = pe.matmul(gu_acc[s % 2][:, k * TOK:(k + 1) * TOK],
                                               lhsT=w[:, c, s * P:(s + 1) * P], rhs=x1_fm[:, c],
                                               start=(c == 0), stop=(c == NC - 1))
                        mm.then_inc(gu_done, 1)
                    if nd.within() and 2 <= s < NM + 2:
                        m = s - 2
                        pe.wait_ge(hid_ready, nd.count(NM, m + 1))
                        if m == 0 and nd.past(1):
                            pe.wait_ge(y_scaled, nd.count(2))
                        for b in range(BATCH):
                            mm = pe.matmul(down_acc[b][:], lhsT=hid[m % RING][:, b * P:(b + 1) * P], rhs=dw[:, m, :],
                                           start=(m == 0), stop=(m == NM - 1))
                        mm.then_inc(down_done, 1)
                    if t.within() and s in (0, 1):
                        b = s
                        if b == 0:
                            pe.wait_ge(x_fm_in[t.par], t.turn(48, 48))
                        if t.past(3):
                            pe.wait_ge(x1_fm_ready, t.count(2, 2 * -3 + b + 1))
                        elif t.past(1):
                            pe.wait_ge(k_cols_ready, t.count(4, 2 * b + 2 - 4))
                        project(t, b, wk, k_projected)
                    if t.within() and s in (3, 4):
                        b = s - 3
                        pe.wait_ge(k_mul, t.count(6, 3 * b + 3))
                        project(t, b, wv, v_projected)
                    if ncc.within() and s == 5:
                        for b in range(BATCH):
                            pe.wait_ge(zn_ready, ncc.count(2, b + 1))
                            if t.within():
                                pe.wait_ge(v_ready, t.count(2, b + 1))
                            else:
                                pe.wait_ge(x1_fm_ready, ncc.count(2, b - 1))
                            turn(z_tok, b, zn_turned)
                    if t.within() and s == 6:
                        for b in range(BATCH):
                            pe.wait_ge(k_ready, t.count(2, b + 1))
                            if ncc.within():
                                pe.wait_ge(zn_fm_ready, ncc.count(8, 4 * b + 4))
                            else:
                                pe.wait_ge(v_ready, t.count(2, b + 1))
                            turn(k_tok, b, k_turned)
                    if ncc.within() and s in (7, 8):
                        b = s - 7
                        if not ncc.past(1):
                            pe.wait_ge(wo_in, 16)
                        pe.wait_ge(zn_fm_ready, ncc.count(8, 4 * b + 4))
                        if t.within():
                            pe.wait_ge(k_cols_ready, t.count(4, 2 * b + 2))
                        for c in range(NC):
                            mm = pe.matmul(work[b][:], lhsT=zn_fm[:, c, b, :], rhs=wo[:, c, :],
                                           start=(c == 0), stop=(c == NC - 1))
                        mm.then_inc(o_done, 1)
                    if ncc.within() and s in (11, 12):
                        b = s - 11
                        pe.wait_ge(x1_ready, ncc.count(2, b + 1))
                        turn(x1_tok[ncc.par], b, x1_turned)

            run(pe, tick)

        @block.vector
        def _(dve):
            def moments_of(norm, n, src):
                for b in range(BATCH):
                    dve.bn_stats(stats[:, norm, b, :], src[:, b, :]).then_inc(stats_done[norm], 1)
                dve.wait_ge(stats_done[norm], n.count(2, 2))
                dve.memset(spare[:], 0.0)
                for b in range(BATCH):
                    dve.bn_aggr(moments[:, norm, b, :], stats[:, norm, b, :]).then_inc(moments_done[norm], 1)
                dve.wait_ge(moments_done[norm], n.count(2, 2))
                dve.tensor_scalar(var_eps[:, norm, :], moments[:, norm, :, 1], LN_EPS, None, ALU.add
                                  ).then_inc(var_done[norm], 1)

            def normalize(norm, n, dst, src, done):
                dve.wait_ge(rstd_done[norm], n.count(1, 1))
                for b in range(BATCH):
                    dve.tensor_scalar(dst[:, b, :], src[:, b, :], moments[:, norm, b, 0:1], rstd[:, norm, b:b + 1],
                                      ALU.subtract, ALU.mult).then_inc(done, 1)

            dve.wait_ge(zeroed, 7)
            dve.wait_ge(small_in, 16 * 7)

            def tick(t):
                nb, ncc, nd = t.back(1), t.back(2), t.back(3)
                for s in range(SLOTS):
                    if nb.within() and s % 2 == 0:
                        i = s // 2
                        if i == 0:
                            dve.wait_ge(rows_in, nb.count(32 * NG, 32 * NG))
                        for j in range(NG // 2):
                            q = slice(j * HEAD, (j + 1) * HEAD)
                            dve.wait_ge(z_done, nb.count(4 * NS, 4 * i + j + 1))
                            dve.tensor_tensor(err[q, 2 * j:2 * j + 2, :, :].rearrange("p g h e -> p (g h e)"),
                                              z_acc[q, 0:2 * P],
                                              v_rows[nb.par][q, i].rearrange("p g c -> p (g c)"),
                                              ALU.subtract).then_inc(err_ready, 1)
                    if nd.within() and 1 <= s <= NM:
                        m = s - 1
                        dve.wait_ge(silu_done, nd.count(NM, m + 1))
                        if m >= RING or nd.past(1):
                            dve.wait_ge(down_done, nd.count(NM, m - RING + 1))
                        dve.scalar_tensor_tensor(hid[m % RING][:], gu_acc[m % 2][:, TOK:2 * TOK],
                                                 up_scale[:, m:m + 1], silu_g[m % 2][:], ALU.mult, ALU.mult
                                                 ).then_inc(hid_ready, 1)
                    if t.within() and s in (1, 2):
                        b = s - 1
                        dve.wait_ge(k_projected, t.count(2, b + 1))
                        if b == 0:
                            dve.wait_ge(x_fm_in[t.par], t.turn(48, 48))
                            if t.past(1):
                                dve.wait_ge(k_stored, t.count(16))
                                dve.wait_ge(k_turned, t.count(2))
                                dve.wait_ge(k_ready, t.count(2))
                        k_in = work[b][:].rearrange("p (h a d) -> p h a d", a=2, d=HEAD // 2)
                        k_si = k_sin[:, b, :].rearrange("p (h a d) -> p h a d", a=2, d=HEAD // 2)
                        H = DM // HEAD
                        dve.tensor_tensor(k_tok[:, b, :].rearrange("p (h d) -> p h d", d=HEAD),
                                          work[b][:].rearrange("p (h d) -> p h d", d=HEAD),
                                          rot[t.par][:, 0:1, :].to_broadcast([P, H, HEAD]), ALU.mult
                                          ).then_inc(k_mul, 1)
                        for a in range(2):
                            table = rot[t.par][:, 1:2, a * HEAD // 2:(a + 1) * HEAD // 2]
                            dve.tensor_tensor(k_si[:, :, a, :], k_in[:, :, 1 - a, :],
                                              table.to_broadcast([P, H, HEAD // 2]), ALU.mult).then_inc(k_mul, 1)
                    if ncc.within() and s == 3:
                        dve.wait_ge(z_tok_in, ncc.count(16, 16))
                        moments_of(0, ncc, z_tok)
                    if ncc.within() and s == 4:
                        normalize(0, ncc, z_tok, z_tok, zn_ready)
                    if t.within() and s == 7:
                        for b in range(BATCH):
                            dve.wait_ge(k_turned, t.count(2, b + 1))
                            if b == 0 and t.past(2):
                                dve.wait_ge(state_added, t.count(4 * NS, -4 * NS))
                            for p in range(2):
                                src = work[b][:].rearrange("p (g a i t) -> p g a i t", a=2, i=NS, t=MB)[:, :, p]
                                dst = k_cols[t.par][:, b * NC:(b + 1) * NC, :, p * MB:(p + 1) * MB].rearrange(
                                    "p (g a) i t -> p g a i t", a=2)[:, :, p]
                                dve.tensor_copy(dst, src).then_inc(k_cols_ready, 1)
                    if ncc.within() and s in (8, 9):
                        b = s - 8
                        if b == 0:
                            dve.wait_ge(x_tok_in, ncc.count(16, 16))
                        dve.wait_ge(o_done, ncc.count(2, b + 1))
                        dve.tensor_tensor(x_tok[:, b, :], work[b][:], x_tok[:, b, :], ALU.add).then_inc(o_added, 1)
                    if ncc.within() and s == 9:
                        dve.wait_ge(o_added, ncc.count(2, 2))
                        moments_of(1, ncc, x_tok)
                    if ncc.within() and s == 10:
                        if ncc.past(2):
                            dve.wait_ge(y_added, ncc.count(2, -2))
                            dve.wait_ge(x1_turned, ncc.count(2, -2))
                        normalize(1, ncc, x1_tok[ncc.par], x_tok, x1_ready)
                    if nd.within() and s == 13:
                        if nd.past(1):
                            dve.wait_ge(out_stored, nd.count(16))
                        for b in range(BATCH):
                            dve.wait_ge(down_done, nd.count(NM, NM))
                            dve.tensor_tensor(y_tok[:, b, :], down_acc[b][:], down_scale[:], ALU.mult
                                              ).then_inc(y_scaled, 1)
                        for b in range(BATCH):
                            dve.wait_ge(y_scaled, nd.count(2, b + 1))
                            dve.tensor_tensor(y_tok[:, b, :], y_tok[:, b, :], x1_tok[nd.par][:, b, :], ALU.add
                                              ).then_inc(y_added, 1)
                        dve.wait_ge(y_added, nd.count(2, 2))
                        moments_of(2, nd, y_tok)
                    if nd.within() and s == 14:
                        normalize(2, nd, y_tok, y_tok, y_ready)

            run(dve, tick)


def rope_table():
    inv = np.float32(1.0) / np.power(np.float32(10000.0), np.arange(0, HEAD, 2, dtype=np.float32) / np.float32(HEAD))
    freqs = np.arange(SEQ, dtype=np.float32)[:, None] * inv.astype(np.float32)[None, :]
    cos, sin = np.cos(freqs), np.sin(freqs)
    return np.concatenate([cos, cos, -sin, sin], axis=1).astype(np.float32)


def kernel(L0_attn_x, L0_attn_Wk, L0_attn_Wv, L0_attn_Wo, L0_attn_ln_gamma, L0_attn_ln_beta, L0_ffn_gate_w,
           L0_ffn_up_w, L0_ffn_down_w, L0_ffn_gate_s, L0_ffn_up_s, L0_ffn_down_s):
    import concourse.bacc as bacc
    from concourse.bass_utils import run_bass_kernel_spmd

    x = np.asarray(L0_attn_x)
    eye = np.eye(P, dtype=np.float32)
    eye_rep = np.zeros((P, NG, HEAD), np.float32)
    for p in range(P):
        eye_rep[p, :, p % HEAD] = -1.0 / STEP
    arrays = {
        "xT": x.transpose(2, 0, 1), "x": x,
        "wkT": np.asarray(L0_attn_Wk).T, "wvT": np.asarray(L0_attn_Wv).T, "woT": np.asarray(L0_attn_Wo).T,
        "gamma": np.asarray(L0_attn_ln_gamma).reshape(NC, P).T, "beta": np.asarray(L0_attn_ln_beta).reshape(NC, P).T,
        "gwT": np.asarray(L0_ffn_gate_w).T, "uwT": np.asarray(L0_ffn_up_w).T, "dwT": np.asarray(L0_ffn_down_w).T,
        "gs": np.asarray(L0_ffn_gate_s).reshape(NM, P).T, "us": np.asarray(L0_ffn_up_s).reshape(NM, P).T,
        "ds_row": np.broadcast_to(np.asarray(L0_ffn_down_s), (P, DM)),
        "rope": rope_table(), "ident": eye, "ident_rep": eye_rep.reshape(P, NG * HEAD),
    }
    arrays = {k: np.ascontiguousarray(v) for k, v in arrays.items()}
    nc = bacc.Bacc("TRN2", target_bir_lowering=False, num_devices=1)
    aps = [nc.dram_tensor(k, v.shape, F32, kind="ExternalInput").ap() for k, v in arrays.items()]
    aps.append(nc.dram_tensor("out", [BATCH, SEQ, DM], F32, kind="ExternalOutput").ap())
    build(nc, *aps)
    r = run_bass_kernel_spmd(nc, [arrays], core_ids=[0])
    return r.results[0]["out"]
```

```python
from contextlib import ExitStack

import numpy as np

import concourse.bass as bass
from concourse import mybir

F32 = mybir.dt.float32
F32R = mybir.dt.float32r
I32 = mybir.dt.int32
U16 = mybir.dt.uint16
ACT = mybir.ActivationFunctionType
ALU = mybir.AluOpType
AX = mybir.AxisListType

P = 128
BATCH, SEQ, DM = 2, 4096, 512
HEAD = 32
MB = 16
NC = DM // P
NG = BATCH * NC
HQ = P // HEAD
NT = SEQ // P
NS = P // MB
INTER = 1408
NM = INTER // P
TOK = BATCH * P
RING = 3
SLOTS = 2 * NS
LN_EPS = 1e-5
STEP = 2.0 / (MB * HEAD)
assert STEP == 2.0 ** -8 and NG * MB == P and NT % 2 == 0


class Nth:

    def __init__(self, off, reg=None):
        self.off, self.reg = off, reg

    def back(self, d):
        return Nth(self.off - d, self.reg)

    def count(self, per, more=0):
        c = per * self.off + more
        return c if self.reg is None else self.reg * (2 * per) + c

    def turn(self, per, more=0):
        c = per * (self.off // 2) + more
        return c if self.reg is None else self.reg * per + c

    def past(self, k):
        return self.reg is not None or self.off >= k

    @property
    def par(self):
        return self.off % 2

    def within(self):
        return self.reg is not None or 0 <= self.off < NT


def build(nc, xT, x, wkT, wvT, woT, gamma, beta, gwT, uwT, dwT, gs, us, ds_row, rope, ident, ident_rep, out):
    with ExitStack() as ctx:
        def sb(name, shape, dt=F32):
            return ctx.enter_context(nc.sbuf_tensor(name, shape, dt))

        def sem(name):
            return ctx.enter_context(nc.semaphore(name))

        k_scr = nc.dram_tensor("k_scr", [BATCH, P, DM], F32, kind="Internal").ap()
        v_scr = nc.dram_tensor("v_scr", [BATCH, P, DM], F32, kind="Internal").ap()
        z_scr = nc.dram_tensor("z_scr", [BATCH, SEQ, DM], F32, kind="Internal").ap()

        gw_scr = nc.dram_tensor("gw_scr", [DM, INTER], F32, kind="Internal").ap()
        uw_scr = nc.dram_tensor("uw_scr", [DM, INTER], F32, kind="Internal").ap()
        dw_scr = nc.dram_tensor("dw_scr", [INTER, DM], F32, kind="Internal").ap()

        wk = sb("wk", [P, NC, DM])
        wv = sb("wv", [P, NC, DM])
        wo = sb("wo", [P, NC, DM])
        gw = sb("gw", [P, NC, INTER], F32R)
        uw = sb("uw", [P, NC, INTER], F32R)
        dw = sb("dw", [P, NM, DM], F32R)
        PIECES = [(w, c, c + 1) for w in (gw, uw) for c in range(NC)] + [(dw, c, min(c + 3, NM)) for c in range(0, NM, 3)]
        low_half = sb("low_half", [P, len(PIECES) + 1])
        low_most = sb("low_most", [P, 1], I32)
        gate_scale = sb("gate_scale", [P, NM])
        up_scale = sb("up_scale", [P, NM])
        down_scale = sb("down_scale", [P, DM])
        ln_gamma = sb("ln_gamma", [P, NC])
        ln_beta = sb("ln_beta", [P, NC])
        eye = sb("eye", [P, P])
        eye_rep = sb("eye_rep", [P, NG, HEAD])
        neg_half = sb("neg_half", [P, BATCH])
        x_fm = [sb(f"x_fm{i}", [P, NC, BATCH, P]) for i in range(2)]
        rot = [sb(f"rot{i}", [P, 2, HEAD]) for i in range(2)]
        k_tok = sb("k_tok", [P, BATCH, DM])
        k_sin = sb("k_sin", [P, DM])
        v_tok = sb("v_tok", [P, BATCH, DM])
        k_rows = [sb(f"k_rows{i}", [P, NS, P]) for i in range(2)]
        v_rows = [sb(f"v_rows{i}", [P, NS, 2, P]) for i in range(2)]
        k_cols = [sb(f"k_cols{i}", [P, NG, NS, 2 * MB]) for i in range(2)]
        err = sb("err", [P, NG, HQ, HEAD])
        state = sb("state", [P, NG, P])
        z_rows = sb("z_rows", [P, NS, 2 * P])
        z_tok = sb("z_tok", [P, BATCH, DM])
        zn_fm = sb("zn_fm", [P, NC, BATCH, P])
        x_tok = sb("x_tok", [P, BATCH, DM])
        x1_tok = [sb(f"x1_tok{i}", [P, BATCH, DM]) for i in range(2)]
        x1_hi = sb("x1_hi", [P, NC, BATCH, P], F32R)
        x1_lo = sb("x1_lo", [P, NC, BATCH, P], F32R)
        silu_g = [sb(f"silu_g{i}", [P, TOK]) for i in range(2)]
        hid = [sb(f"hid{i}", [P, TOK]) for i in range(2)]
        hid_hi = [sb(f"hid_hi{i}", [P, TOK], F32R) for i in range(RING)]
        hid_lo = [sb(f"hid_lo{i}", [P, TOK], F32R) for i in range(RING)]
        y_tok = x_tok
        stats = sb("stats", [P, 3, BATCH, 6])
        moments = sb("moments", [P, 3, BATCH, 2])
        var_eps = sb("var_eps", [P, 3, BATCH])
        spare = sb("spare", [P, 1])
        rstd = sb("rstd", [P, 3, BATCH])

        def bank(name):
            return ctx.enter_context(nc.psum_tensor(name, [P, 512], F32))

        state_acc = bank("state_acc")
        z_acc = bank("z_acc")
        gu_acc = [bank("gu_acc0"), bank("gu_acc1")]
        down_acc = [bank("down_acc0"), bank("down_acc1")]
        work = [bank("work0"), bank("work1")]

        w_in = sem("w_in")
        wo_in = sem("wo_in")
        ffn_copied = sem("ffn_copied")
        ffn_in = sem("ffn_in")
        low_half_max = sem("low_half_max")
        low_half_known = sem("low_half_known")
        small_in = sem("small_in")
        zeroed = sem("zeroed")
        x_fm_in = [sem("x_fm_in0"), sem("x_fm_in1")]
        k_projected = sem("k_projected")
        v_projected = sem("v_projected")
        k_mul = sem("k_mul")
        k_ready = sem("k_ready")
        v_ready = sem("v_ready")
        k_stored = sem("k_stored")
        v_stored = sem("v_stored")
        rows_in = sem("rows_in")
        k_turned = sem("k_turned")
        k_cols_ready = sem("k_cols_ready")
        state_begun = sem("state_begun")
        z_done = sem("z_done")
        z_saved = sem("z_saved")
        err_ready = sem("err_ready")
        state_added = sem("state_added")
        state_ready = sem("state_ready")
        z_stored = sem("z_stored")
        z_tok_in = sem("z_tok_in")
        x_tok_in = sem("x_tok_in")
        stats_done = [sem(f"stats_done{i}") for i in range(3)]
        moments_done = [sem(f"moments_done{i}") for i in range(3)]
        var_done = [sem(f"var_done{i}") for i in range(3)]
        rstd_done = [sem(f"rstd_done{i}") for i in range(3)]
        zn_ready = sem("zn_ready")
        zn_turned = sem("zn_turned")
        zn_fm_ready = sem("zn_fm_ready")
        o_done = sem("o_done")
        o_added = sem("o_added")
        x1_ready = sem("x1_ready")
        x1_turned = sem("x1_turned")
        x1_hi_ready = sem("x1_hi_ready")
        x1_lo_ready = sem("x1_lo_ready")
        gu_done = sem("gu_done")
        silu_done = sem("silu_done")
        hid_ready = sem("hid_ready")
        hid_hi_ready = sem("hid_hi_ready")
        hid_lo_ready = sem("hid_lo_ready")
        down_done = sem("down_done")
        y_scaled = sem("y_scaled")
        y_added = sem("y_added")
        y_ready = sem("y_ready")
        out_stored = sem("out_stored")

        block = ctx.enter_context(nc.Block())

        FIRST, LAST = 4, NT - 2

        def run(eng, tick):
            for t in range(-1, FIRST):
                tick(Nth(t))
            with eng.Fori(FIRST // 2, LAST // 2) as pair:
                tick(Nth(0, pair))
                tick(Nth(1, pair))
            for t in range(LAST, NT + 3):
                tick(Nth(t))

        def rows(n, b=None, first=0, count=P):
            return bass.ds(n.count(P, first), count)

        @block.sync
        def _(sp):
            sp.dma_start(wk[:], wkT.rearrange("(c p) n -> p c n", p=P)).then_inc(w_in, 16)

            def ahead(value):
                if not isinstance(value, int):
                    sp.compute_val(value)
                return value

            def load_x_fm(n, used):
                if n.past(2):
                    sp.wait_ge(v_projected, used)
                for b in range(BATCH):
                    sp.dma_start(x_fm[n.par][:, :, b, :],
                                 xT[:, b, rows(n)].rearrange("(c p) t -> p c t", p=P)).then_inc(x_fm_in[n.par], 16)
                sp.dma_start(rot[n.par][:], rope[rows(n), :].rearrange("t (a d) -> t a d", a=2)
                             ).then_inc(x_fm_in[n.par], 16)

            load_x_fm(Nth(0), 0)
            for dst, src in ((gw_scr, gwT), (uw_scr, uwT), (dw_scr, dwT)):
                sp.dma_start(dst, src).then_inc(ffn_copied, 16)
            sp.dma_start(wv[:], wvT.rearrange("(c p) n -> p c n", p=P)).then_inc(w_in, 16)
            for dst, src in ((gate_scale, gs), (up_scale, us), (down_scale, ds_row), (ln_gamma, gamma),
                             (ln_beta, beta), (eye, ident)):
                sp.dma_start(dst[:], src).then_inc(small_in, 16)
            sp.dma_start(eye_rep[:], ident_rep.rearrange("p (g e) -> p g e", g=NG)).then_inc(small_in, 16)
            sp.dma_start(wo[:], woT.rearrange("(c p) n -> p c n", p=P)).then_inc(wo_in, 16)
            sp.wait_ge(zeroed, 7)

            def store_z(n, half, saved, stored):
                i0 = half * NS // 2
                sp.wait_ge(z_saved, saved)
                for g in range(NG):
                    b, hg = divmod(g, NC)
                    sp.dma_start(z_scr[b, rows(n, first=i0 * MB, count=P // 2), hg * P:(hg + 1) * P]
                                 .rearrange("(i t) c -> t i c", t=MB),
                                 z_rows[g * MB:(g + 1) * MB, i0:i0 + NS // 2, (g % 2) * P:(g % 2 + 1) * P]
                                 ).then_inc(z_stored, 16)
                sp.wait_ge(z_stored, stored)

            def tick(t):
                nb, ncc, nd = t.back(1), t.back(2), t.back(3)
                saved = [ahead(n.count(NS, (half + 1) * NS // 2)) for half, n in enumerate((nb, ncc))]
                z_sent = [ahead(n.count(2 * 16 * NG, (half + 1) * 16 * NG)) for half, n in enumerate((nb, ncc))]
                c_before, x_used, both = ahead(ncc.count(2)), ahead(t.count(2)), ahead(t.count(2, 2))
                scanned, kv_sent = ahead(t.count(4 * NS, -4 * NS)), ahead(t.count(16, 16))
                y_sent = ahead(ncc.count(16, -16))
                rows_sent, y_both = ahead(t.count(32 * NG, 32 * NG)), ahead(nd.count(2, 2))
                if ncc.within():
                    store_z(ncc, 1, saved[1], z_sent[1])
                    if ncc.past(1):
                        sp.wait_ge(zn_turned, c_before)
                        sp.wait_ge(x1_ready, c_before)
                    if ncc.past(2):
                        sp.wait_ge(out_stored, y_sent)
                    sp.dma_start(z_tok[:], z_scr[:, rows(ncc), :].rearrange("b t f -> t b f")).then_inc(z_tok_in, 16)
                    sp.dma_start(x_tok[:], x[:, rows(ncc), :].rearrange("b t f -> t b f")).then_inc(x_tok_in, 16)
                if t.back(-1).within() and t.past(0):
                    load_x_fm(t.back(-1), x_used)
                if t.reg is None and t.off == 0:
                    sp.wait_ge(ffn_copied, 3 * 16)
                    for dst, src in ((gw, gw_scr), (uw, uw_scr), (dw, dw_scr)):
                        sp.dma_start(dst[:].bitcast(F32), src.rearrange("(c p) n -> p c n", p=P)).then_inc(ffn_in, 16)
                if t.within():
                    sp.wait_ge(k_ready, both)
                    sp.dma_start(k_scr.rearrange("b t f -> t b f"), k_tok[:]).then_inc(k_stored, 16)
                    sp.wait_ge(v_ready, both)
                    sp.dma_start(v_scr.rearrange("b t f -> t b f"), v_tok[:]).then_inc(v_stored, 16)
                    if t.past(2):
                        sp.wait_ge(state_added, scanned)
                    for scr, stored in ((k_scr, k_stored), (v_scr, v_stored)):
                        sp.wait_ge(stored, kv_sent)
                        for g in range(NG):
                            b, hg = divmod(g, NC)
                            r = slice(g * MB, (g + 1) * MB)
                            dst = k_rows[t.par][r] if scr is k_scr else v_rows[t.par][r, :, g % 2, :]
                            sp.dma_start(dst, scr[b, :, hg * P:(hg + 1) * P].rearrange("(i t) c -> t i c", t=MB)
                                         ).then_inc(rows_in, 16)
                    sp.wait_ge(rows_in, rows_sent)
                if nb.within():
                    store_z(nb, 0, saved[0], z_sent[0])
                if nd.within():
                    sp.wait_ge(y_ready, y_both)
                    sp.dma_start(out[:, rows(nd), :].rearrange("b t f -> t b f"), y_tok[:]).then_inc(out_stored, 16)

            run(sp, tick)
            sp.wait_ge(out_stored, 16 * NT)

        @block.gpsimd
        def _(pool):
            for buf in (*v_rows, *k_cols, err, state):
                pool.memset(buf[:], 0.0).then_inc(zeroed, 1)
            pool.memset(neg_half[:], -0.5).then_inc(zeroed, 1)
            pool.wait_ge(zeroed, 7)

            def inverse_root(norm, n):
                pool.wait_ge(var_done[norm], n.count(1, 1))
                pool.tensor_tensor(rstd[:, norm, :], var_eps[:, norm, :], neg_half[:], ALU.pow
                                   ).then_inc(rstd_done[norm], 1)

            def tick(t):
                nk, ncc, nd = t.back(-1), t.back(2), t.back(3)
                for s in range(SLOTS):
                    if nd.within() and 2 <= s < NM + 2:
                        m = s - 2
                        pool.wait_ge(hid_hi_ready, nd.count(NM, m + 1))
                        pool.tensor_tensor(hid_lo[m % RING][:], hid[m % 2][:], hid_hi[m % RING][:].bitcast(F32),
                                           ALU.subtract).then_inc(hid_lo_ready, 1)
                    if ncc.within() and s == 3:
                        inverse_root(0, ncc)
                    if ncc.within() and s == 9:
                        inverse_root(1, ncc)
                    if nd.within() and s == 14:
                        inverse_root(2, nd)
                    if t.reg is None and t.off == 2 and s == 13:
                        pool.wait_ge(low_half_max, len(PIECES) + 1)
                        pool.partition_all_reduce(low_most[:], low_half[:, len(PIECES):], P,
                                                  bass.bass_isa.ReduceOp.max).then_inc(low_half_known, 1)
                    if nk.within() and s in (14, 15):
                        b = s - 14
                        pool.wait_ge(k_mul, nk.count(6, 3 * b + 3))
                        pool.tensor_tensor(k_tok[:, b, :], k_tok[:, b, :], k_sin[:], ALU.add
                                           ).then_inc(k_ready, 1)

            run(pool, tick)

        @block.scalar
        def _(act):
            def copy_state():
                for h in range(HQ):
                    q = slice(h * HEAD, (h + 1) * HEAD)
                    act.activation(state[q, :, q], state_acc[q, 0:NG * HEAD].rearrange("p (g e) -> p g e", g=NG),
                                   ACT.Copy, scale=-STEP).then_inc(state_ready, 1)

            act.wait_ge(zeroed, 7)
            act.wait_ge(state_begun, HQ)
            copy_state()
            act.wait_ge(small_in, 16 * 7)

            def tick(t):
                nb, ncc, nd = t.back(1), t.back(2), t.back(3)
                for s in range(SLOTS):
                    i = s // 2
                    if nb.within() and s % 2 == 0:
                        act.wait_ge(err_ready, nb.count(4 * NS, 4 * i + 4))
                        if nb.past(1):
                            act.wait_ge(z_stored, nb.count(32 * NG, -32 * NG + 16 * NG * (1 + i // (NS // 2))))
                        act.activation(z_rows[:, i, :], z_acc[:, 0:2 * P], ACT.Copy
                                       ).then_inc(z_saved, 1)
                    if nb.within() and s % 2 == 1:
                        act.wait_ge(state_added, nb.count(4 * NS, 4 * i + 4))
                        copy_state()
                    if nd.within() and s < NM:
                        act.wait_ge(gu_done, nd.count(NM, s + 1))
                        if s >= 2 or nd.past(1):
                            act.wait_ge(hid_ready, nd.count(NM, s - 1))
                        act.activation(silu_g[s % 2][:], gu_acc[s % 2][:, 0:TOK], ACT.Silu,
                                       scale=gate_scale[:, s:s + 1]).then_inc(silu_done, 1)
                    if nd.within() and 1 <= s <= NM:
                        m = s - 1
                        act.wait_ge(hid_ready, nd.count(NM, m + 1))
                        if m >= RING or nd.past(1):
                            act.wait_ge(down_done, nd.count(NM, m - RING + 1))
                        act.activation(hid_hi[m % RING][:], hid[m % 2][:], ACT.Copy).then_inc(hid_hi_ready, 1)
                    if t.within() and s in (1, 2):
                        b = s - 1
                        act.wait_ge(v_projected, t.count(2, b + 1))
                        if t.past(1):
                            act.wait_ge(v_stored, t.count(16))
                        act.activation(v_tok[:, b, :], work[b][:], ACT.Copy).then_inc(v_ready, 1)
                    if ncc.within() and s == 6:
                        for b in range(BATCH):
                            act.wait_ge(zn_turned, ncc.count(2, b + 1))
                            if ncc.past(1):
                                act.wait_ge(o_done, ncc.count(2))
                            for c in range(NC):
                                act.activation(zn_fm[:, c, b, :], work[b][:, c * P:(c + 1) * P], ACT.Identity,
                                               scale=ln_gamma[:, c:c + 1], bias=ln_beta[:, c:c + 1]
                                               ).then_inc(zn_fm_ready, 1)
                    if ncc.within() and s in (12, 13):
                        b = s - 12
                        act.wait_ge(x1_turned, ncc.count(2, b + 1))
                        if ncc.past(1):
                            act.wait_ge(gu_done, ncc.count(NM))
                        act.activation(x1_hi[:, :, b, :], work[b][:].rearrange("p (c t) -> p c t", c=NC), ACT.Copy
                                       ).then_inc(x1_hi_ready, 1)

            run(act, tick)

        @block.tensor
        def _(pe):
            pe.wait_ge(small_in, 16 * 7)
            pe.wait_ge(zeroed, 7)
            for h in range(HQ):
                q = slice(h * HEAD, (h + 1) * HEAD)
                pe.matmul(state_acc[q, 0:NG * HEAD], lhsT=eye[:, q], rhs=eye_rep[:], start=True, stop=False,
                          skip_group_check=True, tile_position=(0, h * HEAD)).then_inc(state_begun, 1)

            def scan_z(n, i):
                if i == 0:
                    pe.wait_ge(rows_in, n.count(32 * NG, 32 * NG))
                    pe.wait_ge(k_cols_ready, n.count(4, 4))
                pe.wait_ge(state_ready, n.count(4 * NS, 4 * i + 4))
                if i >= 1 or n.past(1):
                    pe.wait_ge(z_saved, n.count(NS, i))
                for g in range(NG):
                    j = g // 2
                    mm = pe.matmul(z_acc[j * HEAD:(j + 1) * HEAD, g % 2 * P:(g % 2 + 1) * P],
                                   lhsT=k_cols[n.par][:, g, i, :], rhs=state[:, g, :], start=True, stop=True,
                                   skip_group_check=True, tile_position=(0, j * HEAD))
                    if g % 2:
                        mm.then_inc(z_done, 1)

            def scan_state(n, i):
                pe.wait_ge(err_ready, n.count(4 * NS, 4 * i + 4))
                for h in range(HQ):
                    q = slice(h * HEAD, (h + 1) * HEAD)
                    pe.matmul(state_acc[q, 0:NG * HEAD], lhsT=k_rows[n.par][:, i, q], rhs=err[:, :, h, :],
                              start=False, stop=False, skip_group_check=True, tile_position=(0, h * HEAD)
                              ).then_inc(state_added, 1)

            def project(n, b, w, done):
                for c in range(NC):
                    mm = pe.matmul(work[b][:], lhsT=x_fm[n.par][:, c, b, :], rhs=w[:, c, :],
                                   start=(c == 0), stop=(c == NC - 1))
                mm.then_inc(done, 1)

            def turn(src, b, done):
                for c in range(NC):
                    mm = pe.transpose(work[b][:, c * P:(c + 1) * P], src[:, b, c * P:(c + 1) * P], eye[:])
                mm.then_inc(done, 1)

            def gate_up(m, dt):
                for k, w in enumerate((gw, uw)):
                    for c in range(NC):
                        for part in (x1_hi, x1_lo):
                            mm = pe.matmul(gu_acc[m % 2][:, k * TOK:(k + 1) * TOK],
                                           lhsT=w[:, c, m * P:(m + 1) * P].bitcast(dt), rhs=part[:, c].bitcast(dt),
                                           start=(c == 0 and part is x1_hi), stop=(c == NC - 1 and part is x1_lo))
                mm.then_inc(gu_done, 1)

            def down(m, dt):
                for b in range(BATCH):
                    for part in (hid_hi, hid_lo):
                        mm = pe.matmul(down_acc[b][:], lhsT=part[m % RING][:, b * P:(b + 1) * P].bitcast(dt),
                                       rhs=dw[:, m, :].bitcast(dt), start=(m == 0 and part is hid_hi),
                                       stop=(m == NM - 1 and part is hid_lo))
                mm.then_inc(down_done, 1)

            inexact = None

            def tick(t):
                nonlocal inexact
                nk, nb, ncc, nd = t.back(-1), t.back(1), t.back(2), t.back(3)
                if t.reg is None and t.off == 3:
                    pe.wait_ge(low_half_known, 1)
                    inexact = pe.value_load(low_most[0:1, 0:1], min_val=0, max_val=0xFFFF)
                for s in range(SLOTS):
                    if nb.within():
                        if s % 2 == 0:
                            scan_z(nb, s // 2)
                        else:
                            scan_state(nb, s // 2)
                    if nd.within() and s < NM:
                        if s == 0:
                            pe.wait_ge(x1_lo_ready, nd.count(2, 2))
                        if s >= 2 or nd.past(1):
                            pe.wait_ge(hid_ready, nd.count(NM, s - 1))
                        with pe.If(inexact == 0):
                            gate_up(s, F32R)
                        with pe.Else():
                            gate_up(s, F32)
                    if nd.within() and 3 <= s < NM + 3:
                        m = s - 3
                        pe.wait_ge(hid_lo_ready, nd.count(NM, m + 1))
                        if m == 0 and nd.past(1):
                            pe.wait_ge(y_scaled, nd.count(2))
                        with pe.If(inexact == 0):
                            down(m, F32R)
                        with pe.Else():
                            down(m, F32)
                    if t.within() and s in (0, 1):
                        b = s
                        pe.wait_ge(k_mul, t.count(6, 3 * b + 3))
                        project(t, b, wv, v_projected)
                    if t.within() and s == 2:
                        for b in range(BATCH):
                            pe.wait_ge(k_ready, t.count(2, b + 1))
                            pe.wait_ge(v_ready, t.count(2, b + 1))
                            turn(k_tok, b, k_turned)
                    if ncc.within() and s == 5:
                        for b in range(BATCH):
                            pe.wait_ge(zn_ready, ncc.count(2, b + 1))
                            if t.within():
                                pe.wait_ge(k_cols_ready, t.count(4, 2 * b + 2))
                            else:
                                pe.wait_ge(x1_lo_ready, ncc.count(2, b - 1))
                            turn(z_tok, b, zn_turned)
                    if ncc.within() and s in (7, 8):
                        b = s - 7
                        if not ncc.past(1):
                            pe.wait_ge(wo_in, 16)
                        pe.wait_ge(zn_fm_ready, ncc.count(8, 4 * b + 4))
                        for c in range(NC):
                            mm = pe.matmul(work[b][:], lhsT=zn_fm[:, c, b, :], rhs=wo[:, c, :],
                                           start=(c == 0), stop=(c == NC - 1))
                        mm.then_inc(o_done, 1)
                    if ncc.within() and s in (11, 12):
                        b = s - 11
                        pe.wait_ge(x1_ready, ncc.count(2, b + 1))
                        turn(x1_tok[ncc.par], b, x1_turned)
                    if nk.within() and s in (13, 14):
                        b = s - 13
                        if b == 0:
                            if not nk.past(1):
                                pe.wait_ge(w_in, 32)
                            pe.wait_ge(x_fm_in[nk.par], nk.turn(48, 48))
                        if ncc.within():
                            pe.wait_ge(x1_lo_ready, ncc.count(2, b + 1))
                        elif t.within():
                            pe.wait_ge(k_cols_ready, t.count(4, 2 * b + 2))
                        project(nk, b, wk, k_projected)

            run(pe, tick)

        @block.vector
        def _(dve):
            def moments_of(norm, n, src):
                for b in range(BATCH):
                    dve.bn_stats(stats[:, norm, b, :], src[:, b, :]).then_inc(stats_done[norm], 1)
                dve.wait_ge(stats_done[norm], n.count(2, 2))
                dve.memset(spare[:], 0.0)
                for b in range(BATCH):
                    dve.bn_aggr(moments[:, norm, b, :], stats[:, norm, b, :]).then_inc(moments_done[norm], 1)
                dve.wait_ge(moments_done[norm], n.count(2, 2))
                dve.tensor_scalar(var_eps[:, norm, :], moments[:, norm, :, 1], LN_EPS, None, ALU.add
                                  ).then_inc(var_done[norm], 1)

            def normalize(norm, n, dst, src, done):
                dve.wait_ge(rstd_done[norm], n.count(1, 1))
                for b in range(BATCH):
                    dve.tensor_scalar(dst[:, b, :], src[:, b, :], moments[:, norm, b, 0:1], rstd[:, norm, b:b + 1],
                                      ALU.subtract, ALU.mult).then_inc(done, 1)

            dve.wait_ge(zeroed, 7)
            dve.wait_ge(small_in, 16 * 7)

            def tick(t):
                nk, nb, ncc, nd = t.back(-1), t.back(1), t.back(2), t.back(3)
                for s in range(SLOTS):
                    if t.reg is None and t.off == 2 and s < len(PIECES):
                        if s == 0:
                            dve.wait_ge(ffn_in, 48)
                        w, c0, c1 = PIECES[s]
                        dve.tensor_reduce(low_half[:, s:s + 1], w[:, c0:c1, :].rearrange("p c n -> p (c n)").bitcast(U16)
                                          [:, 0::2], AX.X, ALU.max).then_inc(low_half_max, 1)
                    if t.reg is None and t.off == 2 and s == len(PIECES):
                        dve.wait_ge(low_half_max, len(PIECES))
                        dve.tensor_reduce(low_half[:, s:s + 1], low_half[:, 0:s], AX.X, ALU.max
                                          ).then_inc(low_half_max, 1)
                    if nb.within() and s % 2 == 0:
                        i = s // 2
                        if i == 0:
                            dve.wait_ge(rows_in, nb.count(32 * NG, 32 * NG))
                        for j in range(NG // 2):
                            q = slice(j * HEAD, (j + 1) * HEAD)
                            dve.wait_ge(z_done, nb.count(4 * NS, 4 * i + j + 1))
                            dve.tensor_tensor(err[q, 2 * j:2 * j + 2, :, :].rearrange("p g h e -> p (g h e)"),
                                              z_acc[q, 0:2 * P],
                                              v_rows[nb.par][q, i].rearrange("p g c -> p (g c)"),
                                              ALU.subtract).then_inc(err_ready, 1)
                    if nd.within() and 1 <= s <= NM:
                        m = s - 1
                        dve.wait_ge(silu_done, nd.count(NM, m + 1))
                        if m >= 2 or nd.past(1):
                            dve.wait_ge(hid_lo_ready, nd.count(NM, m - 1))
                        dve.scalar_tensor_tensor(hid[m % 2][:], gu_acc[m % 2][:, TOK:2 * TOK],
                                                 up_scale[:, m:m + 1], silu_g[m % 2][:], ALU.mult, ALU.mult
                                                 ).then_inc(hid_ready, 1)
                    if ncc.within() and s == 3:
                        dve.wait_ge(z_tok_in, ncc.count(16, 16))
                        moments_of(0, ncc, z_tok)
                    if ncc.within() and s == 4:
                        normalize(0, ncc, z_tok, z_tok, zn_ready)
                    if t.within() and s == 3:
                        for b in range(BATCH):
                            dve.wait_ge(k_turned, t.count(2, b + 1))
                            if b == 0 and t.past(2):
                                dve.wait_ge(state_added, t.count(4 * NS, -4 * NS))
                            for p in range(2):
                                src = work[b][:].rearrange("p (g a i t) -> p g a i t", a=2, i=NS, t=MB)[:, :, p]
                                dst = k_cols[t.par][:, b * NC:(b + 1) * NC, :, p * MB:(p + 1) * MB].rearrange(
                                    "p (g a) i t -> p g a i t", a=2)[:, :, p]
                                dve.tensor_copy(dst, src).then_inc(k_cols_ready, 1)
                    if ncc.within() and s in (8, 9):
                        b = s - 8
                        if b == 0:
                            dve.wait_ge(x_tok_in, ncc.count(16, 16))
                        dve.wait_ge(o_done, ncc.count(2, b + 1))
                        dve.tensor_tensor(x_tok[:, b, :], work[b][:], x_tok[:, b, :], ALU.add).then_inc(o_added, 1)
                    if ncc.within() and s == 9:
                        dve.wait_ge(o_added, ncc.count(2, 2))
                        moments_of(1, ncc, x_tok)
                    if ncc.within() and s == 10:
                        if ncc.past(2):
                            dve.wait_ge(y_added, ncc.count(2, -2))
                            dve.wait_ge(x1_turned, ncc.count(2, -2))
                        normalize(1, ncc, x1_tok[ncc.par], x_tok, x1_ready)
                    if ncc.within() and s in (13, 14):
                        b = s - 13
                        dve.wait_ge(x1_hi_ready, ncc.count(2, b + 1))
                        dve.tensor_tensor(x1_lo[:, :, b, :], work[b][:].rearrange("p (c t) -> p c t", c=NC),
                                          x1_hi[:, :, b, :].bitcast(F32), ALU.subtract).then_inc(x1_lo_ready, 1)
                    if nd.within() and s == 14:
                        if nd.past(1):
                            dve.wait_ge(out_stored, nd.count(16))
                        for b in range(BATCH):
                            dve.wait_ge(down_done, nd.count(NM, NM))
                            dve.tensor_tensor(y_tok[:, b, :], down_acc[b][:], down_scale[:], ALU.mult
                                              ).then_inc(y_scaled, 1)
                        for b in range(BATCH):
                            dve.wait_ge(y_scaled, nd.count(2, b + 1))
                            dve.tensor_tensor(y_tok[:, b, :], y_tok[:, b, :], x1_tok[nd.par][:, b, :], ALU.add
                                              ).then_inc(y_added, 1)
                        dve.wait_ge(y_added, nd.count(2, 2))
                        moments_of(2, nd, y_tok)
                    if nd.within() and s == 15:
                        normalize(2, nd, y_tok, y_tok, y_ready)
                    if nk.within() and s in (14, 15):
                        b = s - 14
                        dve.wait_ge(k_projected, nk.count(2, b + 1))
                        if b == 0:
                            dve.wait_ge(x_fm_in[nk.par], nk.turn(48, 48))
                            if nk.past(1):
                                dve.wait_ge(k_stored, nk.count(16))
                                dve.wait_ge(k_turned, nk.count(2))
                        if b == 1 or nk.past(1):
                            dve.wait_ge(k_ready, nk.count(2, b))
                        k_in = work[b][:].rearrange("p (h a d) -> p h a d", a=2, d=HEAD // 2)
                        k_si = k_sin[:].rearrange("p (h a d) -> p h a d", a=2, d=HEAD // 2)
                        H = DM // HEAD
                        dve.tensor_tensor(k_tok[:, b, :].rearrange("p (h d) -> p h d", d=HEAD),
                                          work[b][:].rearrange("p (h d) -> p h d", d=HEAD),
                                          rot[nk.par][:, 0:1, :].to_broadcast([P, H, HEAD]), ALU.mult
                                          ).then_inc(k_mul, 1)
                        for a in range(2):
                            table = rot[nk.par][:, 1:2, a * HEAD // 2:(a + 1) * HEAD // 2]
                            dve.tensor_tensor(k_si[:, :, a, :], k_in[:, :, 1 - a, :],
                                              table.to_broadcast([P, H, HEAD // 2]), ALU.mult).then_inc(k_mul, 1)

            run(dve, tick)


def rope_table():
    inv = np.float32(1.0) / np.power(np.float32(10000.0), np.arange(0, HEAD, 2, dtype=np.float32) / np.float32(HEAD))
    freqs = np.arange(SEQ, dtype=np.float32)[:, None] * inv.astype(np.float32)[None, :]
    cos, sin = np.cos(freqs), np.sin(freqs)
    return np.concatenate([cos, cos, -sin, sin], axis=1).astype(np.float32)


def kernel(L0_attn_x, L0_attn_Wk, L0_attn_Wv, L0_attn_Wo, L0_attn_ln_gamma, L0_attn_ln_beta, L0_ffn_gate_w,
           L0_ffn_up_w, L0_ffn_down_w, L0_ffn_gate_s, L0_ffn_up_s, L0_ffn_down_s):
    import concourse.bacc as bacc
    from concourse.bass_utils import run_bass_kernel_spmd

    x = np.asarray(L0_attn_x)
    eye = np.eye(P, dtype=np.float32)
    eye_rep = np.zeros((P, NG, HEAD), np.float32)
    for p in range(P):
        eye_rep[p, :, p % HEAD] = -1.0 / STEP
    arrays = {
        "xT": x.transpose(2, 0, 1), "x": x,
        "wkT": np.asarray(L0_attn_Wk).T, "wvT": np.asarray(L0_attn_Wv).T, "woT": np.asarray(L0_attn_Wo).T,
        "gamma": np.asarray(L0_attn_ln_gamma).reshape(NC, P).T, "beta": np.asarray(L0_attn_ln_beta).reshape(NC, P).T,
        "gwT": np.asarray(L0_ffn_gate_w).T, "uwT": np.asarray(L0_ffn_up_w).T, "dwT": np.asarray(L0_ffn_down_w).T,
        "gs": np.asarray(L0_ffn_gate_s).reshape(NM, P).T, "us": np.asarray(L0_ffn_up_s).reshape(NM, P).T,
        "ds_row": np.broadcast_to(np.asarray(L0_ffn_down_s), (P, DM)),
        "rope": rope_table(), "ident": eye, "ident_rep": eye_rep.reshape(P, NG * HEAD),
    }
    arrays = {k: np.ascontiguousarray(v) for k, v in arrays.items()}
    nc = bacc.Bacc("TRN2", target_bir_lowering=False, num_devices=1)
    aps = [nc.dram_tensor(k, v.shape, F32, kind="ExternalInput").ap() for k, v in arrays.items()]
    aps.append(nc.dram_tensor("out", [BATCH, SEQ, DM], F32, kind="ExternalOutput").ap())
    build(nc, *aps)
    r = run_bass_kernel_spmd(nc, [arrays], core_ids=[0])
    return r.results[0]["out"]
```

```python
from contextlib import ExitStack

import numpy as np

import concourse.bass as bass
from concourse import mybir

F32 = mybir.dt.float32
F32R = mybir.dt.float32r
I32 = mybir.dt.int32
U16 = mybir.dt.uint16
ACT = mybir.ActivationFunctionType
ALU = mybir.AluOpType
AX = mybir.AxisListType

P = 128
BATCH, SEQ, DM = 2, 4096, 512
HEAD = 32
MB = 16
NC = DM // P
NG = BATCH * NC
HQ = P // HEAD
NT = SEQ // P
NS = P // MB
INTER = 1408
NM = INTER // P
TOK = BATCH * P
RING = 3
SLOTS = 2 * NS
LN_EPS = 1e-5
STEP = 2.0 / (MB * HEAD)
assert STEP == 2.0 ** -8 and NG * MB == P and NT % 2 == 0


class Nth:

    def __init__(self, off, reg=None):
        self.off, self.reg = off, reg

    def back(self, d):
        return Nth(self.off - d, self.reg)

    def count(self, per, more=0):
        c = per * self.off + more
        return c if self.reg is None else self.reg * (2 * per) + c

    def turn(self, per, more=0):
        c = per * (self.off // 2) + more
        return c if self.reg is None else self.reg * per + c

    def past(self, k):
        return self.reg is not None or self.off >= k

    @property
    def par(self):
        return self.off % 2

    def within(self):
        return self.reg is not None or 0 <= self.off < NT


def build(nc, xT, x, wkT, wvT, woT, gamma, beta, gwT, uwT, dwT, gs, us, ds_row, rope, ident, ident_rep, out):
    with ExitStack() as ctx:
        def sb(name, shape, dt=F32):
            return ctx.enter_context(nc.sbuf_tensor(name, shape, dt))

        def sem(name):
            return ctx.enter_context(nc.semaphore(name))

        k_scr = nc.dram_tensor("k_scr", [2, BATCH, P, DM], F32, kind="Internal").ap()
        v_scr = nc.dram_tensor("v_scr", [2, BATCH, P, DM], F32, kind="Internal").ap()
        z_scr = nc.dram_tensor("z_scr", [BATCH, SEQ, DM], F32, kind="Internal").ap()

        gw_scr = nc.dram_tensor("gw_scr", [DM, INTER], F32, kind="Internal").ap()
        uw_scr = nc.dram_tensor("uw_scr", [DM, INTER], F32, kind="Internal").ap()
        dw_scr = nc.dram_tensor("dw_scr", [INTER, DM], F32, kind="Internal").ap()

        wk = [sb(f"wk{i}", [P, NC, DM], F32R) for i in range(2)]
        wv = [sb(f"wv{i}", [P, NC, DM], F32R) for i in range(2)]
        wo = [sb(f"wo{i}", [P, NC, DM], F32R) for i in range(2)]
        o_bias = sb("o_bias", [P, DM])
        gw = sb("gw", [P, NC, INTER], F32R)
        uw = sb("uw", [P, NC, INTER], F32R)
        dw = sb("dw", [P, NM, DM], F32R)
        PIECES = [(w, c, c + 1) for w in (gw, uw) for c in range(NC)] + [(dw, c, min(c + 3, NM)) for c in range(0, NM, 3)]
        low_half = sb("low_half", [P, len(PIECES) + 1])
        low_most = sb("low_most", [P, 1], I32)
        gate_scale = sb("gate_scale", [P, NM])
        up_scale = sb("up_scale", [P, NM])
        down_scale = sb("down_scale", [P, DM])
        ln_gamma = sb("ln_gamma", [P, NC])
        ln_beta = sb("ln_beta", [P, NC])
        eye = sb("eye", [P, P])
        neg_half = sb("neg_half", [P, BATCH])
        x_fm = sb("x_fm", [P, NC, BATCH, P])
        fm = [sb(f"fm{i}", [P, NC, BATCH, P], F32R) for i in range(2)]
        rot = [sb(f"rot{i}", [P, 2, HEAD]) for i in range(2)]
        k_tok = sb("k_tok", [P, BATCH, DM])
        k_sin = sb("k_sin", [P, DM])
        v_tok = [sb("v_tok", [P, DM]), k_sin]
        k_rows = sb("k_rows", [P, NS, P])
        v_rows = sb("v_rows", [P, NS, 2, P])
        k_cols = [sb(f"k_cols{i}", [P, NG, NS, 2 * MB]) for i in range(2)]
        err = sb("err", [P, NG, HQ, HEAD])
        state = sb("state", [P, NG, P])
        eye_rep = k_rows[:, 0:2, :].rearrange("p i (g e) -> p (i g) e", e=HEAD)
        z_tok = sb("z_tok", [P, BATCH, DM])
        x_tok = sb("x_tok", [P, BATCH, DM])
        x1_tok = [sb(f"x1_tok{i}", [P, BATCH, DM]) for i in range(2)]
        x1_hi = sb("x1_hi", [P, NC, BATCH, P], F32R)
        x1_lo = sb("x1_lo", [P, NC, BATCH, P], F32R)
        hid = [sb(f"hid{i}", [P, TOK]) for i in range(2)]
        hid_hi = [sb(f"hid_hi{i}", [P, TOK], F32R) for i in range(RING)]
        hid_lo = [sb(f"hid_lo{i}", [P, TOK], F32R) for i in range(RING)]
        y_tok = x_tok
        stats = sb("stats", [P, 3, BATCH, 6])
        moments = sb("moments", [P, 3, BATCH, 2])
        var_eps = sb("var_eps", [P, 3, BATCH])
        spare = sb("spare", [P, 1])
        rstd = sb("rstd", [P, 3, BATCH])

        def bank(name):
            return ctx.enter_context(nc.psum_tensor(name, [P, 512], F32))

        state_acc = bank("state_acc")
        z_acc = bank("z_acc")
        gu_acc = [bank("gu_acc0"), bank("gu_acc1")]
        down_acc = [bank("down_acc0"), bank("down_acc1")]
        work = [bank("work0"), bank("work1")]

        wk_in = sem("wk_in")
        wv_in = sem("wv_in")
        wo_in = sem("wo_in")
        w_high = sem("w_high")
        w_low = sem("w_low")
        wo_scaled = sem("wo_scaled")
        bias_done = sem("bias_done")
        bias_ready = sem("bias_ready")
        ffn_copied = sem("ffn_copied")
        ffn_in = [sem("gate_in"), sem("up_in"), sem("down_in")]
        low_half_max = sem("low_half_max")
        low_half_known = sem("low_half_known")
        small_in = sem("small_in")
        zeroed = sem("zeroed")
        x_fm_in = sem("x_fm_in")
        rot_in = [sem("rot_in0"), sem("rot_in1")]
        x_high = sem("x_high")
        x_low = sem("x_low")
        k_projected = sem("k_projected")
        v_projected = sem("v_projected")
        k_mul = sem("k_mul")
        k_ready = sem("k_ready")
        v_ready = sem("v_ready")
        k_stored = sem("k_stored")
        v_stored = sem("v_stored")
        rows_in = [sem("rows_in0"), sem("rows_in1")]
        k_turned = sem("k_turned")
        k_cols_ready = sem("k_cols_ready")
        state_begun = sem("state_begun")
        z_done = sem("z_done")
        z_saved = sem("z_saved")
        err_ready = sem("err_ready")
        state_added = sem("state_added")
        state_ready = sem("state_ready")
        z_stored = sem("z_stored")
        z_tok_in = sem("z_tok_in")
        x_tok_in = sem("x_tok_in")
        stats_done = [sem(f"stats_done{i}") for i in range(3)]
        moments_done = [sem(f"moments_done{i}") for i in range(3)]
        var_done = [sem(f"var_done{i}") for i in range(3)]
        rstd_done = [sem(f"rstd_done{i}") for i in range(3)]
        zn_ready = sem("zn_ready")
        zn_turned = sem("zn_turned")
        zn_high = sem("zn_high")
        zn_low = sem("zn_low")
        x_biased = sem("x_biased")
        o_done = sem("o_done")
        o_added = sem("o_added")
        x1_ready = sem("x1_ready")
        x1_turned = sem("x1_turned")
        x1_hi_ready = sem("x1_hi_ready")
        x1_lo_ready = sem("x1_lo_ready")
        gu_done = sem("gu_done")
        silu_done = sem("silu_done")
        hid_ready = sem("hid_ready")
        hid_hi_ready = sem("hid_hi_ready")
        hid_lo_ready = sem("hid_lo_ready")
        down_done = sem("down_done")
        y_scaled = sem("y_scaled")
        y_added = sem("y_added")
        y_ready = sem("y_ready")
        out_stored = sem("out_stored")

        block = ctx.enter_context(nc.Block())

        FIRST, LAST = 4, NT - 2

        def run(eng, tick, begin=-1):
            for t in range(begin, FIRST):
                tick(Nth(t))
            with eng.Fori(FIRST // 2, LAST // 2) as pair:
                tick(Nth(0, pair))
                tick(Nth(1, pair))
            for t in range(LAST, NT + 4):
                tick(Nth(t))

        def rows(n, b=None, first=0, count=P):
            return bass.ds(n.count(P, first), count)

        @block.sync
        def _(sp):
            def ahead(value):
                if not isinstance(value, int):
                    sp.compute_val(value)
                return value

            def load_x_fm(n, split, used):
                if n.past(1):
                    sp.wait_ge(x_low, split)
                for b in range(BATCH):
                    sp.dma_start(x_fm[:, :, b, :],
                                 xT[:, b, rows(n)].rearrange("(c p) t -> p c t", p=P)).then_inc(x_fm_in, 16)
                if n.past(2):
                    sp.wait_ge(k_mul, used)
                sp.dma_start(rot[n.par][:], rope[rows(n), :].rearrange("t (a d) -> t a d", a=2)
                             ).then_inc(rot_in[n.par], 16)

            for c in range(NC):
                sp.dma_start(x1_tok[c // 2][:, c % 2, :], wkT[c * P:(c + 1) * P, :]).then_inc(wk_in, 16)
            load_x_fm(Nth(0), 0, 0)
            for c in range(NC):
                sp.dma_start((x_tok, z_tok)[c // 2][:, c % 2, :], wvT[c * P:(c + 1) * P, :]).then_inc(wv_in, 16)
            for dst, src in ((gate_scale, gs), (up_scale, us), (down_scale, ds_row), (ln_gamma, gamma),
                             (ln_beta, beta), (eye, ident)):
                sp.dma_start(dst[:], src).then_inc(small_in, 16)
            sp.dma_start(eye_rep, ident_rep.rearrange("p (g e) -> p g e", g=NG)).then_inc(small_in, 16)
            sp.wait_ge(w_low, NC)
            for c in range(NC):
                sp.dma_start(x1_tok[c // 2][:, c % 2, :], woT[c * P:(c + 1) * P, :]).then_inc(wo_in, 16)
            sp.wait_ge(zeroed, 6)
            sp.wait_ge(state_begun, HQ)

            def store_z(n, half, saved, stored):
                i0 = half * NS // 2
                sp.wait_ge(z_saved, saved)
                for g in range(NG):
                    b, hg = divmod(g, NC)
                    sp.dma_start(z_scr[b, rows(n, first=i0 * MB, count=P // 2), hg * P:(hg + 1) * P]
                                 .rearrange("(i t) c -> t i c", t=MB),
                                 v_rows[g * MB:(g + 1) * MB, i0:i0 + NS // 2, g % 2, :]).then_inc(z_stored, 16)
                sp.wait_ge(z_stored, stored)

            def load_rows(par, half, stored_k, stored_v):
                i0 = half * NS // 2
                for scr, stored, done in ((k_scr, k_stored, stored_k), (v_scr, v_stored, stored_v)):
                    sp.wait_ge(stored, done)
                    for g in range(NG):
                        b, hg = divmod(g, NC)
                        r = slice(g * MB, (g + 1) * MB)
                        place = k_rows[r] if scr is k_scr else v_rows[r, :, g % 2, :]
                        sp.dma_start(place[:, i0:i0 + NS // 2, :],
                                     scr[par, b, i0 * MB:i0 * MB + P // 2, hg * P:(hg + 1) * P]
                                     .rearrange("(i t) c -> t i c", t=MB)).then_inc(rows_in[half], 16)

            def load_ffn(i):
                dst, src = ((gw, gw_scr), (uw, uw_scr), (dw, dw_scr))[i]
                sp.wait_ge(ffn_copied, 3 * 16)
                sp.dma_start(dst[:].bitcast(F32), src.rearrange("(c p) n -> p c n", p=P)).then_inc(ffn_in[i], 16)

            def tick(t):
                nb, ncc, ny = t.back(1), t.back(2), t.back(4)
                saved = [ahead(n.count(NS, (half + 1) * NS // 2)) for half, n in enumerate((nb, ncc))]
                z_sent = [ahead(n.count(2 * 16 * NG, (half + 1) * 16 * NG)) for half, n in enumerate((nb, ncc))]
                c_before, split, used = ahead(ncc.count(2)), ahead(t.count(2, 2)), ahead(t.count(6, -3))
                half_scanned, scanned = ahead(nb.count(4 * NS, 2 * NS)), ahead(nb.count(4 * NS))
                k_sent = [ahead(n.count(16, 16)) for n in (t, nb)]
                v_sent = [ahead(n.count(32, 32)) for n in (t, nb)]
                v_first, rows_b = ahead(t.count(2, 1)), ahead(t.count(32 * NG, -32 * NG))
                y_sent, y_both = ahead(ncc.count(16, -16)), ahead(ny.count(2, 2))
                if ncc.within():
                    store_z(ncc, 1, saved[1], z_sent[1])
                    if ncc.past(1):
                        sp.wait_ge(zn_turned, c_before)
                    sp.dma_start(z_tok[:], z_scr[:, rows(ncc), :].rearrange("b t f -> t b f")).then_inc(z_tok_in, 16)
                if nb.within():
                    if nb.past(1):
                        sp.wait_ge(state_added, scanned)
                    load_rows(nb.par, 1, k_sent[1], v_sent[1])
                if ny.within():
                    sp.wait_ge(y_ready, y_both)
                    sp.dma_start(out[:, rows(ny), :].rearrange("b t f -> t b f"), y_tok[:]).then_inc(out_stored, 16)
                if ncc.within():
                    if ncc.past(1):
                        sp.wait_ge(x1_ready, c_before)
                    if ncc.past(2):
                        sp.wait_ge(out_stored, y_sent)
                    sp.dma_start(x_tok[:], x[:, rows(ncc), :].rearrange("b t f -> t b f")).then_inc(x_tok_in, 16)
                if t.back(-1).within() and t.past(0):
                    load_x_fm(t.back(-1), split, used)
                if t.within():
                    if t.past(2):
                        for half in range(2):
                            sp.wait_ge(rows_in[half], rows_b)
                    sp.wait_ge(v_ready, v_first)
                    sp.dma_start(v_scr[t.par, 0], v_tok[0][:]).then_inc(v_stored, 16)
                    sp.wait_ge(k_ready, split)
                    sp.dma_start(k_scr[t.par].rearrange("b t f -> t b f"), k_tok[:]).then_inc(k_stored, 16)
                    sp.wait_ge(v_ready, split)
                    sp.dma_start(v_scr[t.par, 1], v_tok[1][:]).then_inc(v_stored, 16)
                if t.reg is None and t.off in (1, 2):
                    load_ffn(2 * (t.off - 1))
                if nb.within():
                    store_z(nb, 0, saved[0], z_sent[0])
                    sp.wait_ge(state_added, half_scanned)
                if t.within():
                    load_rows(t.par, 0, k_sent[0], v_sent[0])
                if t.reg is None and t.off == 0:
                    for dst, src in ((gw_scr, gwT), (uw_scr, uwT), (dw_scr, dwT)):
                        sp.dma_start(dst, src).then_inc(ffn_copied, 16)
                if t.reg is None and t.off == 1:
                    load_ffn(1)

            run(sp, tick)
            sp.wait_ge(out_stored, 16 * NT)

        @block.gpsimd
        def _(pool):
            for buf in (v_rows, *k_cols, err, state):
                pool.memset(buf[:], 0.0).then_inc(zeroed, 1)
            pool.memset(neg_half[:], -0.5).then_inc(zeroed, 1)
            pool.wait_ge(zeroed, 6)

            def inverse_root(norm, n):
                pool.wait_ge(var_done[norm], n.count(1, 1))
                pool.tensor_tensor(rstd[:, norm, :], var_eps[:, norm, :], neg_half[:], ALU.pow
                                   ).then_inc(rstd_done[norm], 1)

            def add_rotated(n, b):
                pool.wait_ge(k_mul, n.count(6, 3 * b + 3))
                pool.tensor_tensor(k_tok[:, b, :], k_tok[:, b, :], k_sin[:], ALU.add).then_inc(k_ready, 1)

            def tick(t):
                ncc, nd, ny = t.back(2), t.back(3), t.back(4)
                for s in range(SLOTS):
                    if nd.within() and 2 <= s < NM + 2:
                        m = s - 2
                        pool.wait_ge(hid_hi_ready, nd.count(NM, m + 1))
                        pool.tensor_tensor(hid_lo[m % RING][:], hid[m % 2][:], hid_hi[m % RING][:].bitcast(F32),
                                           ALU.subtract).then_inc(hid_lo_ready, 1)
                    if ncc.within() and s == 3:
                        inverse_root(0, ncc)
                    if ncc.within() and s == 9:
                        inverse_root(1, ncc)
                    if nd.within() and s == 14:
                        for b in range(BATCH):
                            pool.wait_ge(y_scaled, nd.count(2, b + 1))
                            pool.tensor_tensor(y_tok[:, b, :], y_tok[:, b, :], x1_tok[nd.par][:, b, :], ALU.add
                                               ).then_inc(y_added, 1)
                    if t.reg is None and t.off == 2 and s == 15:
                        pool.wait_ge(low_half_max, len(PIECES) + 1)
                        pool.partition_all_reduce(low_most[:], low_half[:, len(PIECES):], P,
                                                  bass.bass_isa.ReduceOp.max).then_inc(low_half_known, 1)
                    if t.within() and s in (0, 1):
                        add_rotated(t, s)
                    if ny.within() and s == 1:
                        inverse_root(2, ny)
                    if ncc.within() and s == 5:
                        if not ncc.past(1):
                            pool.wait_ge(bias_ready, 1)
                        pool.wait_ge(x_tok_in, ncc.count(16, 16))
                        for b in range(BATCH):
                            pool.tensor_tensor(x_tok[:, b, :], x_tok[:, b, :], o_bias[:], ALU.add
                                               ).then_inc(x_biased, 1)

            run(pool, tick)

        @block.scalar
        def _(act):
            def copy_state():
                for h in range(HQ):
                    q = slice(h * HEAD, (h + 1) * HEAD)
                    act.activation(state[q, :, q], state_acc[q, 0:NG * HEAD].rearrange("p (g e) -> p g e", g=NG),
                                   ACT.Copy, scale=-STEP).then_inc(state_ready, 1)

            def high_part(w, stage, c):
                act.activation(w[0][:, c, :], stage[c // 2][:, c % 2, :], ACT.Copy).then_inc(w_high, 1)

            act.wait_ge(wk_in, 16 * NC)
            for c in range(NC):
                high_part(wk, x1_tok, c)

            def tick(t):
                nk, nb, ncc, nd = t.back(-1), t.back(1), t.back(2), t.back(3)
                for s in range(SLOTS):
                    i = s // 2
                    if nb.within() and s % 2 == 0:
                        act.wait_ge(err_ready, nb.count(4 * NS, 4 * i + 4))
                        act.activation(v_rows[:, i].rearrange("p g c -> p (g c)"), z_acc[:, 0:2 * P], ACT.Copy
                                       ).then_inc(z_saved, 1)
                    if nb.within() and s % 2 == 1:
                        act.wait_ge(state_added, nb.count(4 * NS, 4 * i + 4))
                        copy_state()
                    if nd.within() and s < NM:
                        act.wait_ge(gu_done, nd.count(NM, s + 1))
                        if s >= 2 or nd.past(1):
                            act.wait_ge(hid_lo_ready, nd.count(NM, s - 1))
                        act.activation(hid[s % 2][:], gu_acc[s % 2][:, 0:TOK], ACT.Silu,
                                       scale=gate_scale[:, s:s + 1]).then_inc(silu_done, 1)
                    if nd.within() and 1 <= s <= NM:
                        m = s - 1
                        act.wait_ge(hid_ready, nd.count(NM, m + 1))
                        if m >= RING or nd.past(1):
                            act.wait_ge(down_done, nd.count(NM, m - RING + 1))
                        act.activation(hid_hi[m % RING][:], hid[m % 2][:], ACT.Copy).then_inc(hid_hi_ready, 1)
                    if t.within() and s in (1, 2):
                        b = s - 1
                        act.wait_ge(v_projected, t.count(2, b + 1))
                        if b == 0 and t.past(1):
                            act.wait_ge(v_stored, t.count(32))
                        if b == 1:
                            act.wait_ge(k_ready, t.count(2, 2))
                        act.activation(v_tok[b][:], work[b][:], ACT.Copy).then_inc(v_ready, 1)
                    if ncc.within() and s == 5:
                        for b in range(BATCH):
                            act.wait_ge(zn_turned, ncc.count(2, b + 1))
                            if t.within():
                                act.wait_ge(v_projected, t.count(2, 2))
                            act.activation(fm[0][:, :, b, :], work[b][:].rearrange("p (c t) -> p c t", c=NC), ACT.Copy
                                           ).then_inc(zn_high, 1)
                    if nk.within() and s in (9, 10):
                        b = s - 9
                        act.wait_ge(x_fm_in, nk.count(32, 32))
                        if nk.past(1):
                            act.wait_ge(v_projected, nk.count(2))
                        if ncc.within():
                            act.wait_ge(o_done, ncc.count(2, 2))
                        act.activation(fm[0][:, :, b, :], x_fm[:, :, b, :], ACT.Copy).then_inc(x_high, 1)
                    if ncc.within() and s in (11, 12):
                        b = s - 11
                        act.wait_ge(x1_turned, ncc.count(2, b + 1))
                        if ncc.past(1):
                            act.wait_ge(gu_done, ncc.count(NM))
                        act.activation(x1_hi[:, :, b, :], work[b][:].rearrange("p (c t) -> p c t", c=NC), ACT.Copy
                                       ).then_inc(x1_hi_ready, 1)
                    if t.reg is None and t.off == 1 and 6 <= s < 6 + NC:
                        act.wait_ge(wo_scaled, s - 5)
                        high_part(wo, x1_tok, s - 6)
                if t.reg is None and t.off == -1:
                    act.wait_ge(wv_in, 16 * NC)
                    for c in range(NC):
                        high_part(wv, (x_tok, z_tok), c)
                    act.wait_ge(zeroed, 6)
                    act.wait_ge(state_begun, HQ)
                    copy_state()
                    act.wait_ge(small_in, 16 * 7)

            run(act, tick)

        @block.tensor
        def _(pe):
            def begin_state():
                pe.wait_ge(small_in, 16 * 7)
                pe.wait_ge(zeroed, 6)
                for h in range(HQ):
                    q = slice(h * HEAD, (h + 1) * HEAD)
                    pe.matmul(state_acc[q, 0:NG * HEAD], lhsT=eye[:, q], rhs=eye_rep, start=True, stop=False,
                              skip_group_check=True, tile_position=(0, h * HEAD)).then_inc(state_begun, 1)

            def scan_z(n, i):
                if i == 0:
                    pe.wait_ge(k_cols_ready, n.count(4, 4))
                pe.wait_ge(state_ready, n.count(4 * NS, 4 * i + 4))
                if i >= 1 or n.past(1):
                    pe.wait_ge(z_saved, n.count(NS, i))
                for g in (*range(0, NG, 2), *range(1, NG, 2)):
                    j = g // 2
                    mm = pe.matmul(z_acc[j * HEAD:(j + 1) * HEAD, g % 2 * P:(g % 2 + 1) * P],
                                   lhsT=k_cols[n.par][:, g, i, :], rhs=state[:, g, :], start=True, stop=True,
                                   skip_group_check=True, tile_position=(0, j * HEAD))
                    if g % 2:
                        mm.then_inc(z_done, 1)

            def scan_state(n, i):
                if i % (NS // 2) == 0:
                    pe.wait_ge(rows_in[i // (NS // 2)], n.count(32 * NG, 32 * NG))
                pe.wait_ge(err_ready, n.count(4 * NS, 4 * i + 4))
                for h in range(HQ):
                    q = slice(h * HEAD, (h + 1) * HEAD)
                    pe.matmul(state_acc[q, 0:NG * HEAD], lhsT=k_rows[:, i, q], rhs=err[:, :, h, :],
                              start=False, stop=False, skip_group_check=True, tile_position=(0, h * HEAD)
                              ).then_inc(state_added, 1)

            def project(b, w, done, c0=0, c1=NC):
                for c in range(c0, c1):
                    for k, (p_x, p_w) in enumerate(((0, 0), (0, 1), (1, 0))):
                        mm = pe.matmul(work[b][:], lhsT=fm[p_x][:, c, b, :], rhs=w[p_w][:, c, :],
                                       start=(c == 0 and k == 0), stop=(c == NC - 1 and k == 2))
                if c1 == NC:
                    mm.then_inc(done, 1)

            def turn(src, b, done):
                for c in range(NC):
                    mm = pe.transpose(work[b][:, c * P:(c + 1) * P], src[:, b, c * P:(c + 1) * P], eye[:])
                mm.then_inc(done, 1)

            def gate_up(m, dt):
                for k, w in enumerate((gw, uw)):
                    for c in range(NC):
                        for part in (x1_hi, x1_lo):
                            mm = pe.matmul(gu_acc[m % 2][:, k * TOK:(k + 1) * TOK],
                                           lhsT=w[:, c, m * P:(m + 1) * P].bitcast(dt), rhs=part[:, c].bitcast(dt),
                                           start=(c == 0 and part is x1_hi), stop=(c == NC - 1 and part is x1_lo))
                mm.then_inc(gu_done, 1)

            def down(m, dt):
                for b in range(BATCH):
                    for part in (hid_hi, hid_lo):
                        mm = pe.matmul(down_acc[b][:], lhsT=part[m % RING][:, b * P:(b + 1) * P].bitcast(dt),
                                       rhs=dw[:, m, :].bitcast(dt), start=(m == 0 and part is hid_hi),
                                       stop=(m == NM - 1 and part is hid_lo))
                mm.then_inc(down_done, 1)

            def tick(t, ffn_dt=None):
                nk, nb, ncc, nd = t.back(-1), t.back(1), t.back(2), t.back(3)
                for s in range(SLOTS):
                    if nb.within():
                        if s % 2 == 0:
                            scan_z(nb, s // 2)
                        else:
                            scan_state(nb, s // 2)
                    if nd.within() and s < NM:
                        if s == 0:
                            pe.wait_ge(x1_lo_ready, nd.count(2, 2))
                        if s >= 2 or nd.past(1):
                            pe.wait_ge(hid_ready, nd.count(NM, s - 1))
                        gate_up(s, ffn_dt)
                    if nd.within() and 3 <= s < NM + 3:
                        m = s - 3
                        pe.wait_ge(hid_lo_ready, nd.count(NM, m + 1))
                        if m == 0 and nd.past(1):
                            pe.wait_ge(y_scaled, nd.count(2))
                        down(m, ffn_dt)
                    if t.within() and s in (1, 2):
                        b = s - 1
                        if b == 0 and not t.past(1):
                            pe.wait_ge(w_low, 2 * NC)
                        pe.wait_ge(k_mul, t.count(6, 3 * b + 3))
                        project(b, wv, v_projected)
                    if t.within() and s == 3:
                        for b in range(BATCH):
                            pe.wait_ge(k_ready, t.count(2, b + 1))
                            pe.wait_ge(v_ready, t.count(2, b + 1))
                            turn(k_tok, b, k_turned)
                    if ncc.within() and s == 5:
                        for b in range(BATCH):
                            pe.wait_ge(zn_ready, ncc.count(2, b + 1))
                            if t.within():
                                pe.wait_ge(k_cols_ready, t.count(4, 2 * b + 2))
                            else:
                                pe.wait_ge(x1_lo_ready, ncc.count(2, b - 1))
                            turn(z_tok, b, zn_turned)
                    if ncc.within() and s in (7, 8):
                        b = s - 7
                        if not ncc.past(1):
                            pe.wait_ge(w_low, 3 * NC)
                        pe.wait_ge(zn_low, ncc.count(2, b + 1))
                        project(b, wo, o_done)
                    if ncc.within() and s in (11, 12):
                        b = s - 11
                        pe.wait_ge(x1_ready, ncc.count(2, b + 1))
                        turn(x1_tok[ncc.par], b, x1_turned)
                    for b, c0, c1 in {13: ((0, 0, 1),), 14: ((0, 1, NC), (1, 0, 1)), 15: ((1, 1, NC),)}.get(s, ()):
                        if not nk.within():
                            continue
                        if c0 == 0:
                            if b == 0 and not nk.past(1):
                                pe.wait_ge(w_low, NC)
                            pe.wait_ge(x_low, nk.count(2, b + 1))
                            if ncc.within():
                                pe.wait_ge(x1_lo_ready, ncc.count(2, b + 1))
                            elif t.within():
                                pe.wait_ge(k_cols_ready, t.count(4, 2 * b + 2))
                        project(b, wk, k_projected, c0, c1)
                    if t.reg is None and t.off == 1 and s == 3:
                        pe.wait_ge(wo_in, 16 * NC)
                        for c in range(NC):
                            mm = pe.matmul(down_acc[0][:], lhsT=ln_beta[:, c:c + 1].to_broadcast([P, P]),
                                           rhs=x1_tok[c // 2][:, c % 2, :], start=(c == 0), stop=(c == NC - 1))
                        mm.then_inc(bias_done, 1)
                if t.reg is None and t.off == -1:
                    begin_state()

            for t in range(-1, 3):
                tick(Nth(t))
            pe.wait_ge(low_half_known, 1)
            inexact = pe.value_load(low_most[0:1, 0:1], min_val=0, max_val=0xFFFF)
            with pe.If(inexact == 0):
                run(pe, lambda t: tick(t, F32R), 3)
            with pe.Else():
                run(pe, lambda t: tick(t, F32), 3)


        @block.vector
        def _(dve):
            def moments_of(norm, n, src):
                for b in range(BATCH):
                    dve.bn_stats(stats[:, norm, b, :], src[:, b, :]).then_inc(stats_done[norm], 1)
                dve.wait_ge(stats_done[norm], n.count(2, 2))
                dve.memset(spare[:], 0.0)
                for b in range(BATCH):
                    dve.bn_aggr(moments[:, norm, b, :], stats[:, norm, b, :]).then_inc(moments_done[norm], 1)
                dve.wait_ge(moments_done[norm], n.count(2, 2))
                dve.tensor_scalar(var_eps[:, norm, :], moments[:, norm, :, 1], LN_EPS, None, ALU.add
                                  ).then_inc(var_done[norm], 1)

            def normalize(norm, n, dst, src, done):
                dve.wait_ge(rstd_done[norm], n.count(1, 1))
                for b in range(BATCH):
                    dve.tensor_scalar(dst[:, b, :], src[:, b, :], moments[:, norm, b, 0:1], rstd[:, norm, b:b + 1],
                                      ALU.subtract, ALU.mult).then_inc(done, 1)

            def low_part(w, stage, c, first):
                dve.wait_ge(w_high, first + c + 1)
                dve.tensor_tensor(w[1][:, c, :], stage[c // 2][:, c % 2, :], w[0][:, c, :].bitcast(F32),
                                  ALU.subtract).then_inc(w_low, 1)

            def rotate(n, b):
                dve.wait_ge(k_projected, n.count(2, b + 1))
                if b == 0:
                    dve.wait_ge(rot_in[n.par], n.turn(16, 16))
                    if n.past(1):
                        dve.wait_ge(k_stored, n.count(16))
                        dve.wait_ge(k_turned, n.count(2))
                        dve.wait_ge(v_stored, n.count(32))
                if b == 1:
                    dve.wait_ge(k_ready, n.count(2, 1))
                heads = DM // HEAD
                k_in = work[b][:].rearrange("p (h a d) -> p h a d", a=2, d=HEAD // 2)
                k_si = k_sin[:].rearrange("p (h a d) -> p h a d", a=2, d=HEAD // 2)
                dve.tensor_tensor(k_tok[:, b, :].rearrange("p (h d) -> p h d", d=HEAD),
                                  work[b][:].rearrange("p (h d) -> p h d", d=HEAD),
                                  rot[n.par][:, 0:1, :].to_broadcast([P, heads, HEAD]), ALU.mult).then_inc(k_mul, 1)
                for a in range(2):
                    table = rot[n.par][:, 1:2, a * HEAD // 2:(a + 1) * HEAD // 2]
                    dve.tensor_tensor(k_si[:, :, a, :], k_in[:, :, 1 - a, :],
                                      table.to_broadcast([P, heads, HEAD // 2]), ALU.mult).then_inc(k_mul, 1)

            for c in range(NC):
                low_part(wk, x1_tok, c, 0)

            def tick(t):
                nk, nb, ncc, nd, ny = t.back(-1), t.back(1), t.back(2), t.back(3), t.back(4)
                for s in range(SLOTS):
                    if nb.within() and s % 2 == 0:
                        i = s // 2
                        if i % (NS // 2) == 0:
                            dve.wait_ge(rows_in[i // (NS // 2)], nb.count(32 * NG, 32 * NG))
                        for j in range(NG // 2):
                            q = slice(j * HEAD, (j + 1) * HEAD)
                            dve.wait_ge(z_done, nb.count(4 * NS, 4 * i + j + 1))
                            dve.tensor_tensor(err[q, 2 * j:2 * j + 2, :, :].rearrange("p g h e -> p (g h e)"),
                                              z_acc[q, 0:2 * P],
                                              v_rows[q, i].rearrange("p g c -> p (g c)"),
                                              ALU.subtract).then_inc(err_ready, 1)
                    if t.reg is None and t.off == 2 and s >= 3:
                        piece = s - 3
                        if piece < len(PIECES):
                            if piece % NC == 0:
                                dve.wait_ge(ffn_in[piece // NC], 16)
                            w, c0, c1 = PIECES[piece]
                            dve.tensor_reduce(low_half[:, piece:piece + 1],
                                              w[:, c0:c1, :].rearrange("p c n -> p (c n)").bitcast(U16)[:, 0::2],
                                              AX.X, ALU.max).then_inc(low_half_max, 1)
                        else:
                            dve.wait_ge(low_half_max, len(PIECES))
                            dve.tensor_reduce(low_half[:, piece:], low_half[:, 0:piece], AX.X, ALU.max
                                              ).then_inc(low_half_max, 1)
                    if nd.within() and 1 <= s <= NM:
                        m = s - 1
                        dve.wait_ge(silu_done, nd.count(NM, m + 1))
                        dve.scalar_tensor_tensor(hid[m % 2][:], gu_acc[m % 2][:, TOK:2 * TOK],
                                                 up_scale[:, m:m + 1], hid[m % 2][:], ALU.mult, ALU.mult
                                                 ).then_inc(hid_ready, 1)
                    if ncc.within() and s == 3:
                        dve.wait_ge(z_tok_in, ncc.count(16, 16))
                        moments_of(0, ncc, z_tok)
                    if ncc.within() and s == 4:
                        normalize(0, ncc, z_tok, z_tok, zn_ready)
                    if t.within() and s == 4:
                        for b in range(BATCH):
                            dve.wait_ge(k_turned, t.count(2, b + 1))
                            if b == 0 and t.past(2):
                                dve.wait_ge(state_added, t.count(4 * NS, -4 * NS))
                            for p in range(2):
                                src = work[b][:].rearrange("p (g a i t) -> p g a i t", a=2, i=NS, t=MB)[:, :, p]
                                dst = k_cols[t.par][:, b * NC:(b + 1) * NC, :, p * MB:(p + 1) * MB].rearrange(
                                    "p (g a) i t -> p g a i t", a=2)[:, :, p]
                                dve.tensor_copy(dst, src).then_inc(k_cols_ready, 1)
                    if ncc.within() and s in (8, 9):
                        b = s - 8
                        dve.wait_ge(x_biased, ncc.count(2, b + 1))
                        dve.wait_ge(o_done, ncc.count(2, b + 1))
                        dve.tensor_tensor(x_tok[:, b, :], work[b][:], x_tok[:, b, :], ALU.add).then_inc(o_added, 1)
                    if ncc.within() and s == 9:
                        dve.wait_ge(o_added, ncc.count(2, 2))
                        moments_of(1, ncc, x_tok)
                    if ncc.within() and s == 10:
                        if ncc.past(2):
                            dve.wait_ge(y_added, ncc.count(2, -2))
                            dve.wait_ge(x1_turned, ncc.count(2, -2))
                        normalize(1, ncc, x1_tok[ncc.par], x_tok, x1_ready)
                    if ncc.within() and s in (12, 13):
                        b = s - 12
                        dve.wait_ge(x1_hi_ready, ncc.count(2, b + 1))
                        dve.tensor_tensor(x1_lo[:, :, b, :], work[b][:].rearrange("p (c t) -> p c t", c=NC),
                                          x1_hi[:, :, b, :].bitcast(F32), ALU.subtract).then_inc(x1_lo_ready, 1)
                    if nd.within() and s == 14:
                        if nd.past(1):
                            dve.wait_ge(out_stored, nd.count(16))
                        for b in range(BATCH):
                            dve.wait_ge(down_done, nd.count(NM, NM))
                            dve.tensor_tensor(y_tok[:, b, :], down_acc[b][:], down_scale[:], ALU.mult
                                              ).then_inc(y_scaled, 1)
                    if ncc.within() and s == 6:
                        for b in range(BATCH):
                            dve.wait_ge(zn_high, ncc.count(2, b + 1))
                            dve.tensor_tensor(fm[1][:, :, b, :], work[b][:].rearrange("p (c t) -> p c t", c=NC),
                                              fm[0][:, :, b, :].bitcast(F32), ALU.subtract).then_inc(zn_low, 1)
                    if nk.within() and s in (10, 11):
                        b = s - 10
                        dve.wait_ge(x_high, nk.count(2, b + 1))
                        dve.tensor_tensor(fm[1][:, :, b, :], x_fm[:, :, b, :], fm[0][:, :, b, :].bitcast(F32),
                                          ALU.subtract).then_inc(x_low, 1)
                    if t.within() and s in (0, 1):
                        rotate(t, s)
                    if ny.within() and s == 1:
                        dve.wait_ge(y_added, ny.count(2, 2))
                        moments_of(2, ny, y_tok)
                    if ny.within() and s == 2:
                        normalize(2, ny, y_tok, y_tok, y_ready)
                    if t.reg is None and t.off == 1:
                        if s == 5:
                            dve.wait_ge(bias_done, 1)
                            dve.tensor_copy(o_bias[:], down_acc[0][:]).then_inc(bias_ready, 1)
                        if 5 <= s < 5 + NC:
                            c = s - 5
                            w = x1_tok[c // 2][:, c % 2, :]
                            dve.tensor_scalar(w, w, ln_gamma[:, c:c + 1], None, ALU.mult).then_inc(wo_scaled, 1)
                        if 7 <= s < 7 + NC:
                            low_part(wo, x1_tok, s - 7, 2 * NC)
                if t.reg is None and t.off == -1:
                    for c in range(NC):
                        low_part(wv, (x_tok, z_tok), c, NC)
                    dve.wait_ge(zeroed, 6)
                    dve.wait_ge(small_in, 16 * 7)

            run(dve, tick)


def rope_table():
    inv = np.float32(1.0) / np.power(np.float32(10000.0), np.arange(0, HEAD, 2, dtype=np.float32) / np.float32(HEAD))
    freqs = np.arange(SEQ, dtype=np.float32)[:, None] * inv.astype(np.float32)[None, :]
    cos, sin = np.cos(freqs), np.sin(freqs)
    return np.concatenate([cos, cos, -sin, sin], axis=1).astype(np.float32)


def kernel(L0_attn_x, L0_attn_Wk, L0_attn_Wv, L0_attn_Wo, L0_attn_ln_gamma, L0_attn_ln_beta, L0_ffn_gate_w,
           L0_ffn_up_w, L0_ffn_down_w, L0_ffn_gate_s, L0_ffn_up_s, L0_ffn_down_s):
    import concourse.bacc as bacc
    from concourse.bass_utils import run_bass_kernel_spmd

    x = np.asarray(L0_attn_x)
    eye = np.eye(P, dtype=np.float32)
    eye_rep = np.zeros((P, NG, HEAD), np.float32)
    for p in range(P):
        eye_rep[p, :, p % HEAD] = -1.0 / STEP
    arrays = {
        "xT": x.transpose(2, 0, 1), "x": x,
        "wkT": np.asarray(L0_attn_Wk).T, "wvT": np.asarray(L0_attn_Wv).T, "woT": np.asarray(L0_attn_Wo).T,
        "gamma": np.asarray(L0_attn_ln_gamma).reshape(NC, P).T, "beta": np.asarray(L0_attn_ln_beta).reshape(NC, P).T,
        "gwT": np.asarray(L0_ffn_gate_w).T, "uwT": np.asarray(L0_ffn_up_w).T, "dwT": np.asarray(L0_ffn_down_w).T,
        "gs": np.asarray(L0_ffn_gate_s).reshape(NM, P).T, "us": np.asarray(L0_ffn_up_s).reshape(NM, P).T,
        "ds_row": np.broadcast_to(np.asarray(L0_ffn_down_s), (P, DM)),
        "rope": rope_table(), "ident": eye, "ident_rep": eye_rep.reshape(P, NG * HEAD),
    }
    arrays = {k: np.ascontiguousarray(v) for k, v in arrays.items()}
    nc = bacc.Bacc("TRN2", target_bir_lowering=False, num_devices=1)
    aps = [nc.dram_tensor(k, v.shape, F32, kind="ExternalInput").ap() for k, v in arrays.items()]
    aps.append(nc.dram_tensor("out", [BATCH, SEQ, DM], F32, kind="ExternalOutput").ap())
    build(nc, *aps)
    r = run_bass_kernel_spmd(nc, [arrays], core_ids=[0])
    return r.results[0]["out"]
```
